# Optimizing a Trainium2 kernel written in Bass

```python
import numpy as np
import jax
import jax.numpy as jnp

def _softmax(x, axis=-1):
    return jax.nn.softmax(x, axis=axis)

def _gelu(x):
    return jax.nn.gelu(x, approximate=True)

def _silu(x):
    return jax.nn.silu(x)

def _sigmoid(x):
    return jax.nn.sigmoid(x)

def _layernorm(x, axis=-1, eps=1e-05):
    m = jnp.mean(x, axis=axis, keepdims=True)
    v = jnp.var(x, axis=axis, keepdims=True)
    return (x - m) / jnp.sqrt(v + eps)

def _scatter_add(tgt, idx, src, axis=0):
    return tgt.at[idx].add(src)

def _segment_sum(src, seg, n):
    return jax.ops.segment_sum(src, seg, n)
kernel_name = 'mk_flamingo_gated_d1_seqx_r4_62d3a2'

def setup_inputs(seed: int=0):
    np.random.seed(seed)
    _w = jnp.asarray

    def _rec_inputs():
        import jax
        import jax.numpy as jnp
        _rk = jax.random.key(seed)
        x = -0.0003929 + 0.9999 * jax.random.normal(jax.random.fold_in(_rk, 1), (32, 100, 512), jnp.float32)
        _lenS = 100 - jax.random.randint(jax.random.fold_in(_rk, 7), (32,), 0, max(1, 100 // 4) + 1, jnp.int32)
        _lenS2 = 361 - jax.random.randint(jax.random.fold_in(_rk, 8), (32,), 0, max(1, 361 // 4) + 1, jnp.int32)
        _ctx_1024P = jax.random.normal(jax.random.fold_in(_rk, 11), (32, 16, 256), jnp.float32)
        _ctx_1024c = jax.random.dirichlet(jax.random.fold_in(_rk, 511), 0.3 * jnp.ones((16,), jnp.float32), (32, 361))
        _ctx_1024t = jnp.einsum('bsk,bkd->bsd', _ctx_1024c, _ctx_1024P)
        _ctx_1024t = _ctx_1024t * jax.lax.rsqrt(jnp.mean(jnp.square(_ctx_1024t)) + 1e-12) * 0.953939
        ctx_1024 = 0.000227908 + 0.99994 * (_ctx_1024t + 0.3 * jax.random.normal(jax.random.fold_in(_rk, 611), (32, 361, 256), jnp.float32))
        _g = jax.random.normal(jax.random.fold_in(_rk, 9001), (2, 1), jnp.float32)
        _g = jnp.sign(_g) * jnp.maximum(jnp.abs(_g), 1.0) + (_g == 0) * 1.0
        g_xattn = _g[0]
        g_ffn = _g[1]
        return (x, ctx_1024, g_xattn, g_ffn)
    x, ctx_1024, g_xattn, g_ffn = _rec_inputs()

    def _L0_xattn_setup():
        import jax, jax.numpy as jnp
        import numpy as np
        EPS = 1e-05

        def rmsnorm(x, g, eps=EPS):
            var = jnp.mean(jnp.square(x), axis=-1, keepdims=True)
            return x * jax.lax.rsqrt(var + eps) * g
        key = jax.random.key(seed)
        ks = jax.random.split(key, 8)
        B, Sq, Skv = (2, 1024, 128)
        dim, cdim, H, D = (512, 256, 16, 128)
        inner = H * D
        s = lambda f: 1.0 / np.sqrt(f)
        return {'hidden_states': jax.random.normal(ks[0], (B, Sq, dim), jnp.float32), 'encoder_hidden_states': jax.random.normal(ks[1], (B, Skv, cdim), jnp.float32), 'Wq': jax.random.normal(ks[2], (dim, inner), jnp.float32) * s(dim), 'Wk': jax.random.normal(ks[3], (cdim, inner), jnp.float32) * s(cdim), 'Wv': jax.random.normal(ks[4], (cdim, inner), jnp.float32) * s(cdim), 'Wo': jax.random.normal(ks[5], (inner, dim), jnp.float32) * s(inner), 'gq': jnp.ones((D,), jnp.float32), 'gk': jnp.ones((D,), jnp.float32)}
    _L0_xattn_all = _L0_xattn_setup()
    _L0_xattn_in = {k: v for k, v in _L0_xattn_all.items() if k in ('Wq', 'Wk', 'Wv', 'Wo', 'gq', 'gk')}
    del _L0_xattn_all

    def _L0_ffn_setup():
        import jax, jax.numpy as jnp
        import numpy as np
        SWIGLU_ALPHA = 1.702
        SWIGLU_LIMIT = 7.0
        B, S, H, E, K, I = (2, 512, 512, 32, 4, 256)
        key = jax.random.key(seed)
        ks = jax.random.split(key, 8)
        return {'hidden_states': jax.random.normal(ks[0], (B, S, H), jnp.float32), 'gate_w': jax.random.normal(ks[1], (E, H), jnp.float32) * 0.02, 'gate_b': jnp.zeros((E,), jnp.float32), 'w_gate': jax.random.normal(ks[2], (E, H, I), jnp.float32) * 0.02, 'b_gate': jnp.zeros((E, I), jnp.float32), 'w_up': jax.random.normal(ks[3], (E, H, I), jnp.float32) * 0.02, 'b_up': jnp.zeros((E, I), jnp.float32), 'w_down': jax.random.normal(ks[4], (E, I, H), jnp.float32) * 0.02, 'b_down': jnp.zeros((E, H), jnp.float32)}
    _L0_ffn_all = _L0_ffn_setup()
    _L0_ffn_in = {k: v for k, v in _L0_ffn_all.items() if k in ('gate_w', 'gate_b', 'w_gate', 'b_gate', 'w_up', 'b_up', 'w_down', 'b_down')}
    del _L0_ffn_all
    return {'x': x, 'ctx_1024': ctx_1024, 'g_xattn': g_xattn, 'g_ffn': g_ffn, 'L0_xattn_Wq': _L0_xattn_in['Wq'], 'L0_xattn_Wk': _L0_xattn_in['Wk'], 'L0_xattn_Wv': _L0_xattn_in['Wv'], 'L0_xattn_Wo': _L0_xattn_in['Wo'], 'L0_xattn_gq': _L0_xattn_in['gq'], 'L0_xattn_gk': _L0_xattn_in['gk'], 'L0_ffn_gate_w': _L0_ffn_in['gate_w'], 'L0_ffn_gate_b': _L0_ffn_in['gate_b'], 'L0_ffn_w_gate': _L0_ffn_in['w_gate'], 'L0_ffn_b_gate': _L0_ffn_in['b_gate'], 'L0_ffn_w_up': _L0_ffn_in['w_up'], 'L0_ffn_b_up': _L0_ffn_in['b_up'], 'L0_ffn_w_down': _L0_ffn_in['w_down'], 'L0_ffn_b_down': _L0_ffn_in['b_down']}

def reference(x, ctx_1024, g_xattn, g_ffn, L0_xattn_Wq, L0_xattn_Wk, L0_xattn_Wv, L0_xattn_Wo, L0_xattn_gq, L0_xattn_gk, L0_ffn_gate_w, L0_ffn_gate_b, L0_ffn_w_gate, L0_ffn_b_gate, L0_ffn_w_up, L0_ffn_b_up, L0_ffn_w_down, L0_ffn_b_down):
    import jax
    import jax.numpy as jnp

    def _L0_xattn_ref(hidden_states, encoder_hidden_states, Wq, Wk, Wv, Wo, gq, gk):
        import jax, jax.numpy as jnp
        import numpy as np
        EPS = 1e-05

        def rmsnorm(x, g, eps=EPS):
            var = jnp.mean(jnp.square(x), axis=-1, keepdims=True)
            return x * jax.lax.rsqrt(var + eps) * g
        B, Sq, _ = hidden_states.shape
        Skv = encoder_hidden_states.shape[1]
        D = gq.shape[0]
        H = Wq.shape[1] // D
        scale = 1.0 / np.sqrt(D)
        q = (hidden_states @ Wq).reshape(B, Sq, H, D)
        k = (encoder_hidden_states @ Wk).reshape(B, Skv, H, D)
        v = (encoder_hidden_states @ Wv).reshape(B, Skv, H, D)
        q = rmsnorm(q, gq)
        k = rmsnorm(k, gk)
        scores = jnp.einsum('bqhd,bkhd->bhqk', q, k) * scale
        attn = jax.nn.softmax(scores, axis=-1)
        out = jnp.einsum('bhqk,bkhd->bqhd', attn, v)
        out = out.reshape(B, Sq, H * D)
        return out @ Wo

    def _L0_ffn_ref(hidden_states, gate_w, gate_b, w_gate, b_gate, w_up, b_up, w_down, b_down):
        import jax, jax.numpy as jnp
        import numpy as np
        SWIGLU_ALPHA = 1.702
        SWIGLU_LIMIT = 7.0
        B, S, H, E, K, I = (2, 512, 512, 32, 4, 256)
        Bb, Ss, Hh = hidden_states.shape
        x = hidden_states.reshape(-1, Hh)
        logits = x @ gate_w.T + gate_b
        topk_logits, topk_idx = jax.lax.top_k(logits, K)
        topk_weight = jax.nn.softmax(topk_logits.astype(jnp.float32), axis=-1)
        flat_idx = topk_idx.reshape(-1)
        xs = jnp.repeat(x, K, axis=0)
        order = jnp.argsort(flat_idx)
        xt = xs[order]
        gid = flat_idx[order]
        group_sizes = jnp.bincount(flat_idx, length=E).astype(jnp.int32)
        gate = jax.lax.ragged_dot(xt, w_gate, group_sizes) + b_gate[gid]
        up = jax.lax.ragged_dot(xt, w_up, group_sizes) + b_up[gid]
        gate = jnp.minimum(gate, SWIGLU_LIMIT)
        up = jnp.clip(up, -SWIGLU_LIMIT, SWIGLU_LIMIT)
        glu = gate * jax.nn.sigmoid(SWIGLU_ALPHA * gate)
        activated = (up + 1.0) * glu
        outs = jax.lax.ragged_dot(activated, w_down, group_sizes) + b_down[gid]
        inv = jnp.argsort(order)
        outs = outs[inv].reshape(-1, K, Hh)
        y = jnp.sum(outs * topk_weight[..., None], axis=1).astype(x.dtype)
        return y.reshape(Bb, Ss, Hh)
    x = x + jnp.tanh(g_xattn[0]) * _L0_xattn_ref(_layernorm(x, axis=-1), ctx_1024, L0_xattn_Wq, L0_xattn_Wk, L0_xattn_Wv, L0_xattn_Wo, L0_xattn_gq, L0_xattn_gk)
    x = x + jnp.tanh(g_ffn[0]) * _L0_ffn_ref(_layernorm(x, axis=-1), L0_ffn_gate_w, L0_ffn_gate_b, L0_ffn_w_gate, L0_ffn_b_gate, L0_ffn_w_up, L0_ffn_b_up, L0_ffn_w_down, L0_ffn_b_down)
    return x

_drawn_inputs = setup_inputs


def setup_inputs(seed=0):
    import zlib

    import numpy as np

    out = dict(_drawn_inputs(seed))
    spreads = {'L0_xattn_gq': (1.0, 0.2),
     'L0_xattn_gk': (1.0, 0.561),
     'L0_ffn_gate_b': (0.0, 0.273),
     'L0_ffn_b_gate': (0.0, 0.8),
     'L0_ffn_b_up': (0.0, 0.8),
     'L0_ffn_b_down': (0.0, 0.1)}
    factors = {'L0_ffn_w_up': 3.275}
    for name, (base, spread) in spreads.items():
        noise = np.random.default_rng([zlib.crc32(name.encode()), seed]).standard_normal(out[name].shape)
        drawn = base * np.exp(spread * noise) if base else spread * noise
        out[name] = jnp.asarray(drawn.astype(out[name].dtype))
    for name, factor in factors.items():
        out[name] = (out[name] * factor).astype(out[name].dtype)
    return out
```

```python
from contextlib import ExitStack

import concourse.bass as bass
from concourse import mybir
from concourse.bass import ds

fp32 = mybir.dt.float32
f32r = mybir.dt.float32r
bf16 = mybir.dt.bfloat16
i32 = mybir.dt.int32
u32 = mybir.dt.uint32
ALU = mybir.AluOpType
ACT = mybir.ActivationFunctionType
X = mybir.AxisListType.X


class Uses:

    def __init__(self, per_pair, pairs):
        self.per_pair, self.pairs, self.count, self.pair = per_pair, pairs, 0, None

    def take(self):
        self.count += 1
        return self.count

    def at(self, use):
        return use if self.pair is None else use + (self.pair - 1) * self.per_pair

    def enter_loop(self, pair):
        self.pair, self.entered = pair, self.count

    def leave_loop(self):
        assert self.count - self.entered == self.per_pair
        self.count += self.per_pair * (self.pairs - 3)
        self.pair = None


def wait_for(eng, sem, value):
    if not isinstance(value, int) or value > 0:
        eng.wait_ge(sem, value)


def flamingo_block(nc, x, ctx, g_xattn, g_ffn, wq, wk, wv, wo, gq, gk,
                   gate_w, gate_b, w_gate, b_gate, w_up, b_up, w_down, b_down, out):
    B, SQ, DM = x.shape
    SK, DC = ctx.shape[1:]
    D = gq.shape[0]
    H = wq.shape[1] // D
    E, _, F = w_gate.shape
    TOPK = 4
    EPS = 1e-5
    PAIRS = B // 2
    GH = 4
    NG = H // GH
    UNITS = 2 * NG
    MC, CC = DM // 128, DC // 128
    KT = -(-SK // 128)
    KROWS = [min(128, SK - 128 * t) for t in range(KT)]
    ctxstack = ExitStack()
    with ctxstack as outer:
        def sem(name):
            return outer.enter_context(nc.semaphore(name))

        def keep(name, shape, dt=fp32):
            return outer.enter_context(nc.sbuf_tensor(name, shape, dt))

        bias_dram = nc.dram_tensor("bias_parts", (E, 3, 2 * F + DM), bf16, kind="Internal").ap()
        xn2_dram = nc.dram_tensor("xn2_rows", (B * SQ, DM), fp32, kind="Internal").ap()

        ident = keep("ident", [128, 128])
        minus_half = keep("minus_half", [128, 16])
        minus_one = keep("minus_one", [128, 4])
        tanh_x = keep("tanh_x", [128, 1])
        tanh_f = keep("tanh_f", [128, 1])
        best = keep("best", [SQ, 8])
        best_index = keep("best_index", [SQ, 8], u32)
        top_value = keep("top_value", [SQ, B, TOPK])
        top_index = keep("top_index", [SQ, B, TOPK], u32)

        attn = ExitStack()

        def sb(name, shape, dt=fp32):
            return attn.enter_context(nc.sbuf_tensor(name, shape, dt))

        wq_sb = sb("wq_sb", [128, MC, H * D])
        whole = ExitStack()
        wk_whole = whole.enter_context(nc.sbuf_tensor("wk_whole", [128, CC, H * D], fp32))
        whole.close()
        wk_lo = sb("wk_lo", [128, CC, H * D], f32r)
        wk_hi = sb("wk_hi", [128, CC, H * D], f32r)
        wv_sb = sb("wv_sb", [128, CC, H * D])
        wo_sb = sb("wo_sb", [128, H, DM])
        gwn_sb = sb("gwn_sb", [E, DM])
        gwT = sb("gwT", [128, MC, E])
        gate_bias = sb("gate_bias", [SQ, E])
        gq_col = sb("gq_col", [D, 1])
        gk_col = sb("gk_col", [D, 1])
        gqk = sb("gqk", [D, 1])
        gx_row = sb("gx_row", [128, 2])
        ones_col = sb("ones_col", [128, 1])
        x_in = sb("x_in", [SQ, 2, DM])
        x_res = sb("x_res", [SQ, 2, DM])
        xn = sb("xn", [SQ, 2, DM])
        xT = sb("xT", [128, MC, 2, SQ])
        ln_stats = sb("ln_stats", [SQ, 2, 2, 6])
        ln_mv = sb("ln_mv", [SQ, 2, 2, 2])
        ln_var = sb("ln_var", [SQ, 2, 2, 1])
        ln_rstd = sb("ln_rstd", [SQ, 2, 2, 1])
        ctx_in = sb("ctx_in", [128, 2, KT, DC])
        ctxT_hi = sb("ctxT_hi", [128, 2, CC, KT * 128], f32r)
        ctxT_lo = sb("ctxT_lo", [128, 2, CC, KT * 128], f32r)
        qT = sb("qT", [128, H, 2, SQ])
        q_sq = sb("q_sq", [128, GH, 2 * SQ])
        q_ss = sb("q_ss", [SQ, GH * 2])
        q_se = sb("q_se", [SQ, GH * 2])
        rq = sb("rq", [SQ, NG, GH, 2])
        k_ss = sb("k_ss", [128, KT, GH])
        k_se = sb("k_se", [128, KT, GH])
        rk = sb("rk", [128, KT, GH])
        kn = sb("kn", [128, KT, GH, D])
        kT = sb("kT", [128, GH, SK])
        s_max = sb("s_max", [SQ, 2, 2])
        s_bias = sb("s_bias", [SQ, 2, 2])
        probs = sb("probs", [SQ, GH, SK])
        p_sum = sb("p_sum", [SQ, GH])
        p_inv = sb("p_inv", [SQ, GH])
        pT = sb("pT", [128, KT, GH * SQ])
        mixT = sb("mixT", [128, CC, GH * SQ])
        oT = sb("oT", [128, H, SQ])
        x1 = sb("x1", [SQ, 2, DM])
        xn2 = sb("xn2", [SQ, 2, DM])
        xn2T = sb("xn2T", [128, MC, SQ])
        logits = sb("logits", [SQ, 2, E])
        attn.close()

        NT = -(-(B * SQ * TOPK + E * 127) // 128)
        XB = 4
        NT += -NT % XB
        NB = 4
        EW = MC * 2 * F + (F // 128) * DM
        FC = F // 128
        moe = ExitStack()

        def sm(name, shape, dt=fp32):
            return moe.enter_context(nc.sbuf_tensor(name, shape, dt))

        w_ring = sm("w_ring", [128, NB, EW])
        b_rows = sm("b_rows", [3, E, 2 * F + DM], bf16)
        ones3 = sm("ones3", [3, 128], bf16)
        t_end_i = sm("t_end_i", [SQ, E], i32)
        tile_tab = sm("tile_tab", [1, 2, NT], i32)
        slot_w = sm("slot_w", [128, NT])
        gather_i = sm("gather_i", [128, NT], u32)
        scatter_i = sm("scatter_i", [128, NT], u32)
        gather_now = sm("gather_now", [128, XB, 1], u32)
        scatter_now = sm("scatter_now", [128, 2, 1], u32)
        routing, tiles = ExitStack(), ExitStack()

        def sr(name, shape, dt=fp32):
            return routing.enter_context(nc.sbuf_tensor(name, shape, dt))

        b_nat = sr("b_nat", [E, 2 * F + DM])
        b_rest = sr("b_rest", [E, 2, 2 * F + DM])
        b_part = sr("b_part", [E, 3, 2 * F + DM], bf16)
        iota_e_i = sr("iota_e_i", [128, E], i32)
        iota_e = sr("iota_e", [128, E])
        iota_l_i = sr("iota_l_i", [128, 128], i32)
        iota_l = sr("iota_l", [128, 128])
        iota_t_i = sr("iota_t_i", [128, NT], i32)
        iota_t = sr("iota_t", [128, NT])
        token_i = sr("token_i", [128, B], i32)
        token_1 = sr("token_1", [128, B])
        before = sr("before", [SQ, SQ])
        ones_sq = sr("ones_sq", [SQ, SQ])
        ones_eb = sr("ones_eb", [SQ, E, B])
        chosen = sr("chosen", [SQ, B, TOPK])
        v_gap = sr("v_gap", [SQ, B, TOPK])
        v_exp = sr("v_exp", [SQ, B, TOPK])
        v_sum = sr("v_sum", [SQ, B, 1])
        v_inv = sr("v_inv", [SQ, B, 1])
        weight = sr("weight", [SQ, B, TOPK])
        hot = sr("hot", [SQ, TOPK, B, E])
        hot_sum = sr("hot_sum", [SQ, B, E])
        count = sr("count", [SQ, E, B])
        run_sum = sr("run_sum", [SQ, E, B])
        n_e = sr("n_e", [SQ, E])
        n_e_i = sr("n_e_i", [SQ, E], i32)
        n_t_i = sr("n_t_i", [SQ, E], i32)
        n_t = sr("n_t", [SQ, E])
        t_end = sr("t_end", [SQ, E])
        shift = sr("shift", [SQ, E])
        place = sr("place", [SQ, B, E])
        wide = sr("wide", [SQ, max(TOPK * B, NT) * E])
        hot_place = wide[:, 0:TOPK * B * E].rearrange("p (k b e) -> p k b e", k=TOPK, b=B)
        tile_cmp = wide[0:1, 0:NT * E].rearrange("p (t e) -> p t e", e=E)
        slot_f = sr("slot_f", [SQ, TOPK, B])
        slot_i = sr("slot_i", [SQ, TOPK, B], i32)
        slot_hi_i = sr("slot_hi_i", [SQ, TOPK, B], i32)
        slot_lo_i = sr("slot_lo_i", [SQ, TOPK, B], i32)
        slot_hi = sr("slot_hi", [SQ, TOPK, B])
        slot_lo = sr("slot_lo", [SQ, TOPK, B])
        NH = 3
        hot_lo = sr("hot_lo", [SQ, NH, 128])
        hot_hi = sr("hot_hi", [SQ, NH, NT])
        hot_val = sr("hot_val", [SQ, NH, 2, NT])
        tile_e = sr("tile_e", [1, NT])
        tile_b = sr("tile_b", [1, NT], i32)
        tile_b_f = sr("tile_b_f", [1, NT])
        slot_tok = sr("slot_tok", [128, NT])
        pad_far = sr("pad_far", [128, NT])
        routing.close()

        def st(name, shape, dt=fp32):
            return tiles.enter_context(nc.sbuf_tensor(name, shape, dt))

        x_tile = st("x_tile", [128, XB, DM])
        xT_tile = st("xT_tile", [128, 2, MC, 128])
        g_min = st("g_min", [128, 2, F])
        u_min = st("u_min", [128, 2, F])
        sig = st("sig", [128, 2, F])
        glu = st("glu", [128, 2, F])
        hid = st("hid", [128, 2, F])
        hidT = st("hidT", [128, 2, FC, 128])
        o_tile = st("o_tile", [128, 2, DM])
        tiles.close()
        moe.close()

        def ps(name, shape):
            return outer.enter_context(nc.psum_tensor(name, shape, fp32))

        ps_k = ps("ps_k", [128, KT, 512])
        ps_act0 = ps("ps_act0", [128, 512])
        ps_s = ps("ps_s", [128, 2, 512])
        ps_act1 = ps("ps_act1", [128, 512])
        ps_dve = ps("ps_dve", [128, 512])
        act_bank = [ps_act0, ps_act1]
        HOT_SUM_STEP = 2 + TOPK + TOPK - 1
        ps_rank = ps_k[0:SQ, 0:2, :].rearrange("p a c -> p (a c)")[:, 0:B * E]
        ps_count = ps_s[0:SQ, :, :].rearrange("p a c -> p (a c)")[:, 0:B * E]
        ps_map = ps_dve
        ps_xT, ps_hT, ps_gu, ps_o = ps_act0, ps_act1, ps_s, [ps_dve, ps_k[:, 0, :]]

        ctx_loaded = [sem(f"ctx_loaded{r}") for r in range(2)]
        x_loaded = [sem(f"x_loaded{r}") for r in range(2)]
        xres_loaded = [sem(f"xres_loaded{r}") for r in range(2)]
        wk_loaded, wq_loaded, wv_loaded, wo_loaded = (sem(f"w{c}_loaded") for c in "kqvo")
        wk_split = sem("wk_split")
        ctxT_rounded = sem("ctxT_rounded")
        small_loaded = sem("small_loaded")
        gatew_loaded = sem("gatew_loaded")
        consts_ready = sem("consts_ready")
        scalars_ready = sem("scalars_ready")
        ctx_free = sem("ctx_free")
        k_full = sem("k_full")
        ksq_ready = sem("ksq_ready")
        kss_ready = sem("kss_ready")
        kse_ready = sem("kse_ready")
        rk_ready = sem("rk_ready")
        kn_ready = sem("kn_ready")
        act_full = sem("act_full")
        act_drained = sem("act_drained")
        dve_full = sem("dve_full")
        dve_drained = sem("dve_drained")
        qse_ready = sem("qse_ready")
        rq_ready = sem("rq_ready")
        s_full = sem("s_full")
        smax_ready = sem("smax_ready")
        sbias_ready = sem("sbias_ready")
        exp_done = sem("exp_done")
        pinv_ready = sem("pinv_ready")
        probs_ready = sem("probs_ready")
        bn_ready = [sem(f"bn_ready{k}") for k in (1, 2)]
        mv_ready = [sem(f"mv_ready{k}") for k in (1, 2)]
        var_ready = [sem(f"var_ready{k}") for k in (1, 2)]
        rstd_ready = [sem(f"rstd_ready{k}") for k in (1, 2)]
        xn_ready = sem("xn_ready")
        xn2_ready = sem("xn2_ready")
        x1_stored = [sem(f"x1_stored{r}") for r in range(2)]
        xn2_stored = [sem(f"xn2_stored{r}") for r in range(2)]
        logits_ready = sem("logits_ready")
        best_ready = sem("best_ready")
        top_ready = sem("top_ready")

        picks_done = sem("picks_done")
        gaps_exp = sem("gaps_exp")
        ranks_full = sem("ranks_full")
        hots_ready = sem("hots_ready")
        vals_ready = sem("vals_ready")
        map_step = sem("map_step")
        moe_consts = sem("moe_consts")
        moe_floats = sem("moe_floats")
        bias_step = sem("bias_step")
        bias_loaded = sem("bias_loaded")
        bias_stored = sem("bias_stored")
        rows_loaded = sem("rows_loaded")
        table_ready = sem("table_ready")
        w_loaded = sem("w_loaded")
        idx_copied = sem("idx_copied")
        sidx_copied = sem("sidx_copied")
        x_gathered = [sem(f"x_gathered{r}") for r in range(XB)]
        xT_full = sem("xT_full")
        xT_drained = sem("xT_drained")
        gu_full = sem("gu_full")
        g_ready = sem("g_ready")
        gu_drained = sem("gu_drained")
        sig_ready = sem("sig_ready")
        glu_ready = sem("glu_ready")
        hid_ready = sem("hid_ready")
        hT_full = sem("hT_full")
        hT_drained = sem("hT_drained")
        o_full = sem("o_full")
        o_drained = sem("o_drained")
        pool_turns = sem("pool_turns")
        dve_turns = sem("dve_turns")
        sp_turns = sem("sp_turns")
        added = sem("added")

        ACT_USES = UNITS * (GH + KT + CC) + 2 * NG
        DVE_USES = UNITS + 2 * 3 + NG + 2 * CC + 2

        class Span:

            def __init__(self, pair, prev, cur, nxt):
                self.pair, self.prev, self.cur, self.nxt = pair, prev, cur, nxt

            def unit(self, k):
                return self.prev if k < 0 else self.cur

            def batch(self, r):
                return self.prev if r < 0 else (self.cur if r < 2 else self.nxt)

        def run(eng, steps, uses=()):
            for l in range(UNITS):
                steps(Span(0, False, True, True), l)
            with eng.Fori(1, PAIRS - 1) as pair:
                for u in uses:
                    u.enter_loop(pair)
                for l in range(UNITS):
                    steps(Span(pair, True, True, True), l)
            for u in uses:
                u.leave_loop()
            for l in range(UNITS):
                steps(Span(PAIRS - 1, True, True, False), l)
            for l in range(NG + 1):
                steps(Span(PAIRS, True, False, False), l)

        def rows(dram, batch):
            return dram[ds(batch, 1), :, :].rearrange("o s d -> (o s) d")

        def ctx_rows_in(eng, batch, slot):
            full = SK // 128
            src = rows(ctx, batch)
            eng.dma_start(ctx_in[:, slot, 0:full, :],
                          src[0:full * 128, :].rearrange("(t p) c -> p t c", p=128)).then_inc(ctx_loaded[slot], 16)
            eng.dma_start(ctx_in[0:KROWS[-1], slot, full, :], src[full * 128:SK, :]).then_inc(ctx_loaded[slot], 16)

        def attention_stored(eng):
            for r in range(2):
                eng.wait_ge(x1_stored[r], 16 * PAIRS)
                eng.wait_ge(xn2_stored[r], 16 * PAIRS)

        block = outer.enter_context(nc.Block())

        def expert_tiles(eng, stage):
            stage(0, 0, (True, False, True))
            for j in range(1, XB):
                stage(j, j, (True, True, True))
            with eng.Fori(1, NT // XB - 1) as q:
                for i in range(XB):
                    stage(XB * q + i, i, (True, True, True))
            for i in range(XB):
                stage(NT - XB + i, i, (True, True, i < XB - 1))
            stage(NT, 0, (False, True, False))

        @block.sync
        def _(sp):
            ctx_rows_in(sp, 0, 0)
            for r in range(2):
                sp.dma_start(x_in[:, r, :], rows(x, r)).then_inc(x_loaded[r], 16)
            sp.dma_start(wq_sb[:], wq.rearrange("(c p) n -> p c n", p=128)).then_inc(wq_loaded, 16)
            sp.dma_start(wk_whole[:], wk.rearrange("(c p) n -> p c n", p=128)).then_inc(wk_loaded, 16)
            sp.dma_start(wv_sb[:], wv.rearrange("(c p) n -> p c n", p=128)).then_inc(wv_loaded, 16)
            sp.dma_start(wo_sb[:], wo.rearrange("(h p) n -> p h n", p=128)).then_inc(wo_loaded, 16)

            def residual_rows_in(p, r):
                wait_for(sp, x1_stored[r], 16 * p)
                wait_for(sp, xn2_stored[r], 16 * p)
                sp.dma_start(x_res[:, r, :], rows(x, 2 * p + r)).then_inc(xres_loaded[r], 16)

            def steps(s, l):
                p = s.pair
                if l == 0 and s.cur:
                    residual_rows_in(p, 0)
                if l == 1:
                    if s.cur:
                        wait_for(sp, ctx_free, 2 * p)
                        ctx_rows_in(sp, 2 * p + 1, 1)
                    if s.nxt:
                        for r in range(2):
                            wait_for(sp, xn_ready, 2 * p + r + 1)
                            sp.dma_start(x_in[:, r, :], rows(x, 2 * p + 2 + r)).then_inc(x_loaded[r], 16)
                if l == 4 and s.cur:
                    residual_rows_in(p, 1)
                if l == 5 and s.nxt:
                    wait_for(sp, ctx_free, 2 * p + 1)
                    ctx_rows_in(sp, 2 * p + 2, 0)
                for at, rel in ((2, -1), (6, 0)):
                    if l == at and s.batch(rel):
                        sp.wait_ge(bn_ready[1], 2 * p + rel + 1)
                        sp.dma_start(rows(out, 2 * p + rel), x1[:, rel % 2, :]).then_inc(x1_stored[rel % 2], 16)
                for at, rel in ((3, -1), (7, 0)):
                    if l == at and s.batch(rel):
                        sp.wait_ge(xn2_ready, 2 * p + rel + 1)
                        sp.dma_start(xn2_dram[ds((2 * p + rel) * SQ, SQ), :], xn2[:, rel % 2, :])\
                          .then_inc(xn2_stored[rel % 2], 16)

            run(sp, steps)
            sp.wait_ge(top_ready, 2 * B)
            attention_stored(sp)
            for part, src in ((slice(0, F), b_gate), (slice(F, 2 * F), b_up), (slice(2 * F, 2 * F + DM), b_down)):
                sp.dma_start(b_nat[:, part], src).then_inc(bias_loaded, 16)

            def load_expert(e, buf):
                gu = w_ring[:, buf, 0:MC * 2 * F].rearrange("p (c n) -> p c n", c=MC)
                sp.dma_start(gu[:, :, 0:F], w_gate[ds(e, 1), :, :].rearrange("o (c p) n -> p (o c) n", p=128))\
                  .then_inc(w_loaded, 16)
                sp.dma_start(gu[:, :, F:2 * F], w_up[ds(e, 1), :, :].rearrange("o (c p) n -> p (o c) n", p=128))\
                  .then_inc(w_loaded, 16)
                sp.dma_start(w_ring[:, buf, MC * 2 * F:EW].rearrange("p (c n) -> p c n", c=FC),
                             w_down[ds(e, 1), :, :].rearrange("o (c p) n -> p (o c) n", p=128)).then_inc(w_loaded, 16)
                sp.wait_ge(w_loaded, 48 * (e + 1))
                sp.sem_inc(sp_turns, 1)

            for e in range(NB):
                load_expert(e, e)
                if e == 0:
                    sp.wait_ge(bias_step, 5)
                    sp.dma_start(bias_dram, b_part[:]).then_inc(bias_stored, 16)
                    sp.wait_ge(bias_stored, 16)
                    sp.dma_start(b_rows[:], bias_dram.rearrange("e s n -> s e n")).then_inc(rows_loaded, 16)
            sp.sem_inc(o_full, 1)
            sp.wait_ge(table_ready, 1)
            with sp.Fori(1, E // NB) as q:
                for j in range(NB):
                    done = sp.value_load(t_end_i[0:1, ds(q * NB + (j - NB), 1)], min_val=1, max_val=NT + 1)
                    sp.wait_ge(o_full, done)
                    load_expert(q * NB + j, j)
            sp.wait_ge(added, 16 * NT)

        @block.gpsimd
        def _(pool):
            pool.dma_start(gq_col[:], gq.rearrange("(p o) -> p o", o=1)).then_inc(small_loaded, 16)
            pool.dma_start(gk_col[:], gk.rearrange("(p o) -> p o", o=1)).then_inc(small_loaded, 16)
            pool.dma_start(gx_row[:, 0:1], g_xattn.partition_broadcast(128)).then_inc(small_loaded, 16)
            pool.dma_start(gx_row[:, 1:2], g_ffn.partition_broadcast(128)).then_inc(small_loaded, 16)
            pool.dma_start(gate_bias[:], gate_b.partition_broadcast(SQ)).then_inc(small_loaded, 16)
            pool.dma_start(gwn_sb[:], gate_w).then_inc(gatew_loaded, 16)
            pool.memset(ident[:], 0.0).then_inc(consts_ready, 1)
            pool.memset(minus_half[:], -0.5).then_inc(consts_ready, 1)
            pool.memset(minus_one[:], -1.0).then_inc(consts_ready, 1)
            pool.memset(ones_col[:], 1.0).then_inc(consts_ready, 1)
            pool.memset(ctxT_hi[:, :, :, SK:].bitcast(i32), 0).then_inc(consts_ready, 1)
            pool.memset(ctxT_lo[:, :, :, SK:].bitcast(i32), 0).then_inc(consts_ready, 1)
            pool.wait_ge(consts_ready, 6)
            pool.affine_select(out=ident[:], in_=ident[:], compare_op=ALU.not_equal, fill=1.0, base=0,
                               pattern=[[-1, 128]], channel_multiplier=1).then_inc(consts_ready, 1)

            def norm_root(kind, batch, r):
                pool.wait_ge(mv_ready[kind], batch + 1)
                pool.sem_inc(pool_turns, 1)
                pool.tensor_scalar(ln_var[:, kind, r, :], ln_mv[:, kind, r, 1:2], EPS, None, ALU.add)\
                    .then_inc(var_ready[kind], 1)
                pool.wait_ge(var_ready[kind], batch + 1)
                pool.tensor_tensor(ln_rstd[:, kind, r, :], ln_var[:, kind, r, :], minus_half[0:SQ, 0:1], ALU.pow)\
                    .then_inc(rstd_ready[kind], 1)

            def query_root(n, g):
                pool.wait_ge(qse_ready, n)
                pool.tensor_tensor(rq[:, g, :, :].rearrange("p h r -> p (h r)"), q_se[:],
                                   minus_half[0:SQ, 0:2 * GH], ALU.pow).then_inc(rq_ready, 1)

            for r in range(2):
                norm_root(0, r, r)
            query_root(1, 0)

            def steps(s, l):
                p = s.pair
                n = UNITS * p + l
                if s.cur:
                    pool.wait_ge(kss_ready, n + 1)
                    pool.sem_inc(pool_turns, 1)
                    pool.tensor_scalar(k_se[:], k_ss[:], D * EPS, None, ALU.add).then_inc(kse_ready, 1)
                    pool.wait_ge(kse_ready, n + 1)
                    pool.tensor_tensor(rk[:].rearrange("p t h -> p (t h)"), k_se[:].rearrange("p t h -> p (t h)"),
                                       minus_half[:, 0:KT * GH], ALU.pow).then_inc(rk_ready, 1)
                if l == 7 and s.nxt:
                    query_root(NG * p + 5, 0)
                if l in (0, 1, 2) and s.cur:
                    query_root(NG * p + l + 2, l + 1)
                for at, rel in ((2, -1), (6, 0)):
                    if l == at and s.batch(rel):
                        norm_root(1, 2 * p + rel, rel % 2)
                for at, r in ((2, 0), (3, 1)):
                    if l == at and s.nxt:
                        norm_root(0, 2 * p + 2 + r, r)
                if s.unit(l - 1):
                    u = n - 1
                    for hp in range(2):
                        pool.wait_ge(exp_done, GH * u + 2 * hp + 2)
                        pool.tensor_tensor(p_inv[:, 2 * hp:2 * hp + 2], p_sum[:, 2 * hp:2 * hp + 2],
                                           minus_one[0:SQ, 0:2], ALU.pow).then_inc(pinv_ready, 1)
                        pool.wait_ge(pinv_ready, 2 * u + hp + 1)
                        pr = probs[:, 2 * hp:2 * hp + 2, :]
                        pool.tensor_tensor(pr, pr, p_inv[:, 2 * hp:2 * hp + 2].unsqueeze(2)
                                           .broadcast_to([SQ, 2, SK]), ALU.mult).then_inc(probs_ready, 1)

            run(pool, steps)

            pool.wait_ge(top_ready, 2 * B)
            attention_stored(pool)
            pool.iota(iota_e_i[:], pattern=[[1, E]], base=0, channel_multiplier=0).then_inc(moe_consts, 1)
            pool.iota(iota_l_i[:], pattern=[[1, 128]], base=0, channel_multiplier=0).then_inc(moe_consts, 1)
            pool.iota(iota_t_i[:], pattern=[[1, NT]], base=0, channel_multiplier=0).then_inc(moe_consts, 1)
            pool.iota(token_i[:], pattern=[[SQ, B]], base=1, channel_multiplier=1).then_inc(moe_consts, 1)
            pool.memset(before[:], 1.0).then_inc(moe_consts, 1)
            pool.memset(ones_sq[:], 1.0).then_inc(moe_consts, 1)
            pool.memset(ones_eb[:], 1.0).then_inc(moe_consts, 1)
            pool.memset(ones3[:], 1.0).then_inc(moe_consts, 1)
            pool.wait_ge(moe_consts, 8)
            pool.affine_select(out=before[:], in_=before[:], compare_op=ALU.is_gt, fill=0.0, base=0,
                               pattern=[[1, SQ]], channel_multiplier=-1).then_inc(moe_consts, 1)
            pool.wait_ge(bias_loaded, 48)
            pool.tensor_copy(b_part[:, 0, :], b_nat[:]).then_inc(bias_step, 1)
            pool.wait_ge(bias_step, 1)
            pool.tensor_tensor(b_rest[:, 0, :], b_nat[:], b_part[:, 0, :], ALU.subtract).then_inc(bias_step, 1)
            pool.wait_ge(bias_step, 2)
            pool.tensor_copy(b_part[:, 1, :], b_rest[:, 0, :]).then_inc(bias_step, 1)
            pool.wait_ge(bias_step, 3)
            pool.tensor_tensor(b_rest[:, 1, :], b_rest[:, 0, :], b_part[:, 1, :], ALU.subtract).then_inc(bias_step, 1)
            pool.wait_ge(bias_step, 4)
            pool.tensor_copy(b_part[:, 2, :], b_rest[:, 1, :]).then_inc(bias_step, 1)

            pool.wait_ge(table_ready, 1)

            def gather(j, i):
                wait_for(pool, xT_full, j - XB + 1)
                pool.tensor_copy(gather_now[:, i, :], gather_i[:, ds(j, 1)]).then_inc(idx_copied, 1)
                pool.wait_ge(idx_copied, j + 1)
                pool.sem_inc(pool_turns, 1)
                pool.indirect_dma_start(out=x_tile[:, i, :], out_offset=None, in_=xn2_dram,
                                        in_offset=bass.IndirectOffsetOnAxis(ap=gather_now[:, i, :], axis=0))\
                    .then_inc(x_gathered[i], 16)

            def add_rows(j, i):
                pool.tensor_copy(scatter_now[:, i % 2, :], scatter_i[:, ds(j, 1)]).then_inc(sidx_copied, 1)
                pool.wait_ge(sidx_copied, j + 1)
                pool.wait_ge(o_drained, j + 1)
                wait_for(pool, added, 16 * j)
                pool.sem_inc(pool_turns, 1)
                pool.indirect_dma_start(out=out.rearrange("b s d -> (b s) d"),
                                        out_offset=bass.IndirectOffsetOnAxis(ap=scatter_now[:, i % 2, :], axis=0),
                                        in_=o_tile[:, i % 2, :], in_offset=None, bounds_check=B * SQ - 1,
                                        oob_is_err=False, compute_op=ALU.add).then_inc(added, 16)

            AHEAD = 5
            for j in range(AHEAD):
                gather(j, j % XB)
            for j in range(XB):
                add_rows(j, j)
                gather(j + AHEAD, (j + AHEAD) % XB)
            with pool.Fori(1, (NT - AHEAD) // XB) as q:
                for i in range(XB):
                    add_rows(XB * q + i, i)
                    gather(XB * q + i + AHEAD, (i + AHEAD) % XB)
            for j in range((NT - AHEAD) // XB * XB, NT):
                add_rows(j, j % XB)
                if j + AHEAD < NT:
                    gather(j + AHEAD, (j + AHEAD) % XB)
            pool.wait_ge(added, 16 * NT)

        @block.scalar
        def _(act):
            act.wait_ge(small_loaded, 16 * 5)
            act.activation(tanh_x[:], gx_row[:, 0:1], ACT.Tanh).then_inc(scalars_ready, 1)
            act.activation(tanh_f[:], gx_row[:, 1:2], ACT.Tanh).then_inc(scalars_ready, 1)
            act.wait_ge(scalars_ready, 4)
            uses = Uses(ACT_USES, PAIRS)

            def drain(dst, src, width, scale=None):
                u = uses.take()
                act.wait_ge(act_full, uses.at(u))
                bank = act_bank[u % 2]
                act.activation(dst, src(bank), ACT.Copy, **({} if scale is None else {"scale": scale}))\
                   .then_inc(act_drained, 1)

            def drain_queries(g, t):
                u = uses.take()
                act.wait_ge(act_full, uses.at(u))
                bank = act_bank[u % 2]
                h = GH * g + 2 * t
                act.activation(qT[:, h:h + 2, :, :].rearrange("p h r q -> p (h r q)"), bank[:, 0:4 * SQ], ACT.Copy,
                               scale=gqk[:, 0:1])
                act.activation(q_sq[:, 2 * t:2 * t + 2, :].rearrange("p h q -> p (h q)"), bank[:, 0:4 * SQ],
                               ACT.Square).then_inc(act_drained, 1)

            for g in range(2):
                for t in range(2):
                    drain_queries(g, t)

            def steps(s, l):
                p = s.pair
                n = UNITS * p + l
                def drain_probs(t):
                    drain(pT[0:KROWS[t], t, :], lambda bank: bank[0:KROWS[t], 0:GH * SQ], GH * SQ)

                def drain_keys(h):
                    drain(kT[:, h, :], lambda bank: bank[:, 0:SK], SK)

                def drain_mix(c):
                    drain(mixT[:, c, :], lambda bank: bank[:, 0:GH * SQ], GH * SQ)

                def exponentials(hp):
                    u, g, r = n - 1, (l - 1) % NG, (l - 1) % UNITS // NG
                    act.wait_ge(sbias_ready, 2 * u + hp + 1)
                    for j in range(2):
                        h = 2 * hp + j
                        act.activation(probs[:, h, :], ps_s[0:SQ, j, 0:SK], ACT.Exp,
                                       bias=s_bias[:, hp, j:j + 1], scale=rq[:, g, h, r:r + 1],
                                       accum_out=p_sum[:, h:h + 1]).then_inc(exp_done, 1)

                new, mid, old = s.cur, s.unit(l - 1), s.unit(l - 2)
                if mid:
                    for h in range(GH):
                        drain_keys(h)
                if old:
                    drain_probs(0)
                if new:
                    act.wait_ge(k_full, n + 1)
                    act.activation(kn[:].rearrange("p t h d -> p (t h d)"),
                                   ps_k[:].rearrange("p t c -> p (t c)"), ACT.Square).then_inc(ksq_ready, 1)
                if old:
                    for t in range(1, KT):
                        drain_probs(t)
                if mid:
                    exponentials(0)
                if old:
                    for c in range(CC):
                        drain_mix(c)
                if (l in (6, 7) and s.nxt) or (l in (0, 1) and s.cur):
                    for t in range(2):
                        drain_queries({6: 0, 7: 1, 0: 2, 1: 3}[l], t)
                if mid:
                    exponentials(1)

            run(act, steps, [uses])

            act.wait_ge(picks_done, 2)
            act.activation(v_exp[:], v_gap[:], ACT.Exp).then_inc(gaps_exp, 1)

            def values(m, j):
                k, b = m // B, m % B
                act.wait_ge(hots_ready, 2 * m + 2)
                wait_for(act, map_step, m - NH + 1)
                act.activation(hot_val[:, j, 0, :], hot_hi[:, j, :], ACT.Copy, scale=token_1[0:SQ, b:b + 1])\
                   .then_inc(vals_ready, 1)
                act.activation(hot_val[:, j, 1, :], hot_hi[:, j, :], ACT.Copy, scale=weight[:, b, k:k + 1])\
                   .then_inc(vals_ready, 1)

            for m in range(TOPK * B):
                values(m, m % NH)

            act.wait_ge(table_ready, 1)

            def stage(j, i, has):
                r = i % 2
                if has[1]:
                    act.wait_ge(hT_full, j)
                    act.activation(hidT[:, 1 - r, :, :].rearrange("p c n -> p (c n)"), ps_hT[:, 0:F], ACT.Copy)\
                       .then_inc(hT_drained, 1)
                if has[2]:
                    act.wait_ge(xT_full, j + 2)
                    act.activation(xT_tile[:, 1 - r, :, :].rearrange("p c n -> p (c n)"), ps_xT[:, 0:DM], ACT.Copy)\
                       .then_inc(xT_drained, 1)
                if has[0]:
                    act.wait_ge(g_ready, j + 1)
                    act.activation(sig[:, r, :], g_min[:, r, :], ACT.Sigmoid, scale=1.702).then_inc(sig_ready, 1)
                if has[1]:
                    act.wait_ge(o_full, j + 1)
                    wait_for(act, added, 16 * (j - 2))
                    act.activation(o_tile[:, 1 - r, :], ps_o[1 - r][:], ACT.Copy, scale=slot_w[:, ds(j - 1, 1)])\
                       .then_inc(o_drained, 1)

            act.wait_ge(xT_full, 1)
            act.activation(xT_tile[:, 0, :, :].rearrange("p c n -> p (c n)"), ps_xT[:, 0:DM], ACT.Copy)\
               .then_inc(xT_drained, 1)
            expert_tiles(act, stage)

        @block.vector
        def _(dve):
            dve.wait_ge(small_loaded, 16 * 5)
            dve.tensor_scalar(gqk[:], gq_col[:], gk_col[:, 0:1], None, ALU.mult).then_inc(scalars_ready, 1)
            dve.wait_ge(scalars_ready, 3)
            dve.tensor_scalar(gqk[:], gqk[:], float(D) ** 0.5, None, ALU.mult).then_inc(scalars_ready, 1)
            dve.wait_ge(scalars_ready, 4)
            uses = Uses(DVE_USES, PAIRS)

            def next_full():
                u = uses.take()
                dve.wait_ge(dve_full, uses.at(u))

            def norm_stats(kind, batch, r, src):
                dve.bn_stats(ln_stats[:, kind, r, :], src).then_inc(bn_ready[kind], 1)
                dve.wait_ge(bn_ready[kind], batch + 1)
                dve.sem_inc(dve_turns, 1)
                dve.bn_aggr(ln_mv[:, kind, r, :], ln_stats[:, kind, r, :]).then_inc(mv_ready[kind], 1)

            def normalise(kind, batch, r, dst, src, done):
                dve.wait_ge(rstd_ready[kind], batch + 1)
                dve.tensor_scalar(dst, src, ln_mv[:, kind, r, 0:1], ln_rstd[:, kind, r, 0:1],
                                  ALU.subtract, ALU.mult).then_inc(done, 1)

            def drain_ctxT(slot, batch):
                for c in range(CC):
                    next_full()
                    dve.tensor_copy(ctxT_hi[:, slot, c, 0:SK], ps_dve[:, 0:SK]).then_inc(ctxT_rounded, 1)
                    dve.wait_ge(ctxT_rounded, CC * batch + c + 1)
                    dve.tensor_tensor(ctxT_lo[:, slot, c, 0:SK], ps_dve[:, 0:SK],
                                      ctxT_hi[:, slot, c, 0:SK].bitcast(fp32), ALU.subtract).then_inc(dve_drained, 1)

            def drain_xT(r):
                next_full()
                dve.tensor_copy(xT[:, :, r, :], ps_dve[:, 0:MC * SQ].rearrange("p (c q) -> p c q", c=MC))\
                   .then_inc(dve_drained, 1)

            def drain_query_sums(group):
                next_full()
                wait_for(dve, rq_ready, group)
                dve.tensor_copy(q_ss[:], ps_dve[0:SQ, 0:2 * GH]).then_inc(dve_drained, 1)
                dve.wait_ge(dve_drained, uses.at(uses.count))
                dve.tensor_scalar(q_se[:], q_ss[:], D * EPS, None, ALU.add).then_inc(qse_ready, 1)

            next_full()
            dve.tensor_copy(gwT[:].rearrange("p c e -> p (c e)"), ps_dve[:, 0:MC * E]).then_inc(dve_drained, 1)
            drain_ctxT(0, 0)
            for r in range(2):
                dve.wait_ge(x_loaded[r], 16)
                norm_stats(0, r, r, x_in[:, r, :])
                normalise(0, r, r, xn[:, r, :], x_in[:, r, :], xn_ready)
            for r in range(2):
                drain_xT(r)
            dve.wait_ge(wk_loaded, 16)
            dve.tensor_copy(wk_hi[:], wk_whole[:]).then_inc(wk_split, 1)
            dve.wait_ge(wk_split, 1)
            dve.tensor_tensor(wk_lo[:], wk_whole[:], wk_hi[:].bitcast(fp32), ALU.subtract).then_inc(wk_split, 1)
            drain_query_sums(0)

            def steps(s, l):
                p = s.pair
                n = UNITS * p + l
                def maxima(hp):
                    u, g, r = n - 1, (l - 1) % NG, (l - 1) % UNITS // NG
                    dve.wait_ge(s_full, 2 * u + hp + 1)
                    dve.tensor_reduce(s_max[:, hp, :], ps_s[0:SQ, :, 0:SK], X, ALU.max).then_inc(smax_ready, 1)
                    dve.wait_ge(smax_ready, 2 * u + hp + 1)
                    dve.scalar_tensor_tensor(s_bias[:, hp, :], s_max[:, hp, :], -1.0,
                                             rq[:, g, 2 * hp:2 * hp + 2, r], ALU.mult, ALU.mult)\
                       .then_inc(sbias_ready, 1)

                if (l == 7 and s.nxt) or (l in (0, 1, 2) and s.cur):
                    drain_query_sums(NG * p + (l + 1) % UNITS if l < 7 else NG * (p + 1))
                for at, rel in ((3, -1), (7, 0)):
                    if l == at and s.batch(rel):
                        next_full()
                        dve.tensor_copy(xn2T[:].rearrange("p c q -> p (c q)"), ps_dve[:, 0:MC * SQ])\
                           .then_inc(dve_drained, 1)
                for at, rel in ((0, -2), (4, -1)):
                    if l == at and s.batch(rel):
                        b, r = 2 * p + rel, rel % 2
                        next_full()
                        dve.tensor_tensor(logits[:, r, :], ps_dve[0:SQ, 0:E], gate_bias[:], ALU.add)\
                           .then_inc(dve_drained, 1)
                        dve.wait_ge(dve_drained, uses.at(uses.count))
                        dve.sem_inc(dve_turns, 1)
                        dve.max(best[:], logits[:, r, :]).then_inc(best_ready, 1)
                        dve.wait_ge(best_ready, 2 * b + 1)
                        dve.sem_inc(dve_turns, 1)
                        dve.max_index(best_index[:], best[:], logits[:, r, :]).then_inc(best_ready, 1)
                        dve.tensor_copy(top_value[:, ds(b, 1), :].rearrange("p o k -> p (o k)"), best[:, 0:TOPK])\
                           .then_inc(top_ready, 1)
                        dve.wait_ge(best_ready, 2 * b + 2)
                        dve.tensor_copy(top_index[:, ds(b, 1), :].rearrange("p o k -> p (o k)"), best_index[:, 0:TOPK])\
                           .then_inc(top_ready, 1)
                for at, r in ((4, 0), (5, 1)):
                    if l == at and s.nxt:
                        drain_xT(r)
                if (l == 3 and s.cur) or (l == 7 and s.nxt):
                    drain_ctxT((l // NG + 1) % 2, 2 * p + (l + 1) // NG)
                if s.cur:
                    dve.wait_ge(ksq_ready, n + 1)
                    dve.tensor_reduce(k_ss[:], kn[:], X, ALU.add).then_inc(kss_ready, 1)
                if s.unit(l - 1):
                    dve.wait_ge(rq_ready, (NG * p + (l - 1) % NG + 1) if l > 0 else NG * p)
                    maxima(0)
                for at, rel in ((2, -1), (6, 0)):
                    if l == at and s.batch(rel):
                        b, r = 2 * p + rel, rel % 2
                        next_full()
                        dve.wait_ge(xres_loaded[r], 16 * (p + rel // 2 + 1))
                        dve.scalar_tensor_tensor(x1[:, r, :], ps_dve[0:SQ, :], tanh_x[0:SQ, 0:1], x_res[:, r, :],
                                                 ALU.mult, ALU.add).then_inc(dve_drained, 1)
                        dve.wait_ge(dve_drained, uses.at(uses.count))
                        norm_stats(1, b, r, x1[:, r, :])
                for at, r in ((2, 0), (3, 1)):
                    if l == at and s.nxt:
                        dve.wait_ge(x_loaded[r], 16 * (p + 2))
                        norm_stats(0, 2 * p + 2 + r, r, x_in[:, r, :])
                if s.cur:
                    dve.wait_ge(rk_ready, n + 1)
                    dve.tensor_tensor(kn[:].rearrange("p t h d -> p (t h) d"),
                                      ps_k[:].rearrange("p t (h d) -> p (t h) d", h=GH),
                                      rk[:].rearrange("p t h -> p (t h)").unsqueeze(2)
                                      .broadcast_to([128, KT * GH, D]), ALU.mult).then_inc(kn_ready, 1)
                for at, r in ((2, 0), (3, 1)):
                    if l == at and s.nxt:
                        normalise(0, 2 * p + 2 + r, r, xn[:, r, :], x_in[:, r, :], xn_ready)
                for at, rel in ((2, -1), (6, 0)):
                    if l == at and s.batch(rel):
                        r = rel % 2
                        normalise(1, 2 * p + rel, r, xn2[:, r, :], x1[:, r, :], xn2_ready)
                if s.unit(l - 1):
                    maxima(1)
                if s.unit(l - 2):
                    g = (l - 2) % NG
                    next_full()
                    dve.tensor_copy(oT[:, GH * g:GH * g + GH, :].rearrange("p h q -> p (h q)"),
                                    ps_dve[:, 0:GH * SQ]).then_inc(dve_drained, 1)

            run(dve, steps, [uses])

            step = [0]

            def then(ins):
                step[0] += 1
                ins.then_inc(picks_done, 1)
                dve.wait_ge(picks_done, step[0])

            dve.wait_ge(top_ready, 2 * B)
            attention_stored(dve)
            then(dve.tensor_copy(chosen[:], top_index[:]))
            then(dve.tensor_tensor(v_gap[:], top_value[:],
                                   top_value[:, :, 0:1].broadcast_to([SQ, B, TOPK]), ALU.subtract))
            dve.wait_ge(moe_consts, 9)
            dve.tensor_copy(iota_e[:], iota_e_i[:]).then_inc(moe_floats, 1)
            dve.tensor_copy(iota_l[:], iota_l_i[:]).then_inc(moe_floats, 1)
            dve.tensor_copy(iota_t[:], iota_t_i[:]).then_inc(moe_floats, 1)
            dve.tensor_copy(token_1[:], token_i[:]).then_inc(moe_floats, 1)
            dve.wait_ge(moe_floats, 4)
            for k in range(TOPK):
                then(dve.tensor_tensor(hot[:, k, :, :], iota_e[0:SQ, :].unsqueeze(1).broadcast_to([SQ, B, E]),
                                       chosen[:, :, k:k + 1].broadcast_to([SQ, B, E]), ALU.is_equal))
            then(dve.tensor_tensor(hot_sum[:], hot[:, 0, :, :], hot[:, 1, :, :], ALU.add))
            then(dve.tensor_tensor(hot_sum[:], hot_sum[:], hot[:, 2, :, :], ALU.add))
            then(dve.tensor_tensor(hot_sum[:], hot_sum[:], hot[:, 3, :, :], ALU.add))
            assert step[0] == HOT_SUM_STEP
            dve.wait_ge(gaps_exp, 1)
            then(dve.tensor_reduce(v_sum[:], v_exp[:], X, ALU.add))
            then(dve.reciprocal(v_inv[:], v_sum[:]))
            then(dve.scalar_tensor_tensor(weight[:], v_exp[:], tanh_f[0:SQ, 0:1],
                                          v_inv[:].broadcast_to([SQ, B, TOPK]), ALU.mult, ALU.mult))
            dve.wait_ge(ranks_full, 2)
            then(dve.tensor_copy(count[:], ps_count.rearrange("p (b e) -> p e b", b=B)))
            then(dve.tensor_tensor_scan(run_sum[:].rearrange("p e b -> p (e b)"),
                                        ones_eb[:].rearrange("p e b -> p (e b)"),
                                        count[:].rearrange("p e b -> p (e b)"), 0.0, ALU.mult, ALU.add))
            then(dve.tensor_tensor(count[:], run_sum[:], count[:], ALU.subtract))
            then(dve.tensor_tensor(n_e[:], run_sum[:, :, B - 1], count[:, :, 0], ALU.subtract))
            then(dve.tensor_scalar(n_e_i[:], n_e[:], 127.0, None, ALU.add))
            then(dve.tensor_scalar(n_t_i[:], n_e_i[:], 7, None, ALU.arith_shift_right))
            then(dve.tensor_copy(n_t[:], n_t_i[:]))
            then(dve.tensor_tensor_scan(t_end[:], ones_eb[:, :, 0], n_t[:], 0.0, ALU.mult, ALU.add))
            then(dve.tensor_tensor(shift[:], t_end[:], n_t[:], ALU.subtract))
            then(dve.scalar_tensor_tensor(shift[:], shift[:], 128.0, count[:, :, 0], ALU.mult, ALU.subtract))
            then(dve.tensor_tensor(count[:], count[:], shift[:].unsqueeze(2).broadcast_to([SQ, E, B]), ALU.add))
            then(dve.tensor_tensor(place[:], ps_rank.rearrange("p (b e) -> p b e", b=B),
                                   count[:].rearrange("p e b -> p b e"), ALU.add))
            for k in range(TOPK):
                then(dve.tensor_tensor(hot_place[:, k, :, :], hot[:, k, :, :], place[:], ALU.mult))
            then(dve.tensor_reduce(slot_f[:], hot_place, X, ALU.add))
            then(dve.tensor_copy(slot_i[:], slot_f[:]))
            then(dve.tensor_scalar(slot_hi_i[:], slot_i[:], 7, None, ALU.arith_shift_right))
            then(dve.tensor_scalar(slot_lo_i[:], slot_i[:], 127, None, ALU.bitwise_and))
            then(dve.tensor_copy(slot_hi[:], slot_hi_i[:]))
            then(dve.tensor_copy(slot_lo[:], slot_lo_i[:]))
            for m in range(TOPK * B):
                k, b, j = m // B, m % B, m % NH
                wait_for(dve, map_step, m - NH + 1)
                dve.tensor_scalar(hot_lo[:, j, :], iota_l[0:SQ, :], slot_lo[:, k, b:b + 1], None, ALU.is_equal)\
                   .then_inc(hots_ready, 1)
                dve.tensor_scalar(hot_hi[:, j, :], iota_t[0:SQ, :], slot_hi[:, k, b:b + 1], None, ALU.is_equal)\
                   .then_inc(hots_ready, 1)
            then(dve.tensor_tensor(tile_cmp, t_end[0:1, :].unsqueeze(1).broadcast_to([1, NT, E]),
                                   iota_t[0:1, :].unsqueeze(2).broadcast_to([1, NT, E]), ALU.is_le))
            then(dve.tensor_reduce(tile_e[:], tile_cmp, X, ALU.add))
            then(dve.tensor_scalar(tile_tab[:, 0, :], tile_e[:], float(E - 1), None, ALU.min))
            then(dve.tensor_scalar(tile_b[:], tile_tab[:, 0, :], NB - 1, None, ALU.bitwise_and))
            then(dve.tensor_copy(tile_b_f[:], tile_b[:]))
            then(dve.tensor_scalar(tile_tab[:, 1, :], tile_b_f[:], float(EW), None, ALU.mult))
            then(dve.tensor_scalar(t_end_i[:], t_end[:], 1.0, None, ALU.add))
            dve.wait_ge(map_step, TOPK * B)
            then(dve.tensor_copy(slot_tok[:], ps_map[:, 0:NT]))
            then(dve.tensor_copy(slot_w[:], ps_map[:, NT:2 * NT]))
            then(dve.tensor_scalar(gather_i[:], slot_tok[:], -1.0, 0.0, ALU.add, ALU.max))
            then(dve.tensor_scalar(pad_far[:], slot_tok[:], 0.0, float(2 ** 20), ALU.is_equal, ALU.mult))
            then(dve.scalar_tensor_tensor(slot_tok[:], slot_tok[:], -1.0, pad_far[:], ALU.add, ALU.add))
            dve.tensor_copy(scatter_i[:], slot_tok[:]).then_inc(table_ready, 1)

            def stage(j, i, has):
                r = i % 2
                if not has[0]:
                    return
                dve.wait_ge(gu_full, j + 1)
                dve.tensor_scalar(g_min[:, r, :], ps_gu[:, r, 0:F], 7.0, None, ALU.min).then_inc(g_ready, 1)
                dve.tensor_scalar(u_min[:, r, :], ps_gu[:, r, F:2 * F], 1.0, 8.0, ALU.add, ALU.min)\
                   .then_inc(gu_drained, 1)
                dve.wait_ge(sig_ready, j + 1)
                dve.tensor_tensor(glu[:, r, :], g_min[:, r, :], sig[:, r, :], ALU.mult).then_inc(glu_ready, 1)
                dve.wait_ge(glu_ready, j + 1)
                dve.wait_ge(gu_drained, j + 1)
                dve.scalar_tensor_tensor(hid[:, r, :], u_min[:, r, :], -6.0, glu[:, r, :], ALU.max, ALU.mult)\
                   .then_inc(hid_ready, 1)

            expert_tiles(dve, stage)

        @block.tensor
        def _(pe):
            mm = nc.tensor.matmul
            acts, dves = Uses(ACT_USES, PAIRS), Uses(DVE_USES, PAIRS)

            def act_use():
                u = acts.take()
                wait_for(pe, act_drained, acts.at(u - 2))
                return act_bank[u % 2]

            def dve_use():
                u = dves.take()
                wait_for(pe, dve_drained, dves.at(u - 1))
                return ps_dve

            def transpose(dst, src, size):
                return nc.tensor.transpose(dst, src, ident[0:size, 0:size])

            def transpose_ctx(slot, batch_of_slot, c):
                pe.wait_ge(ctx_loaded[slot], 32 * (batch_of_slot + 1))
                bank = dve_use()
                for t in range(KT):
                    rows_ = KROWS[t]
                    last = transpose(bank[:, 128 * t:128 * t + rows_],
                                     ctx_in[0:rows_, slot, t, 128 * c:128 * c + 128], rows_)
                last.then_inc(dve_full, 1)

            def transpose_x(r, batch):
                pe.wait_ge(xn_ready, batch + 1)
                bank = dve_use()
                for c in range(MC):
                    last = transpose(bank[:, SQ * c:SQ * c + SQ], xn[:, r, 128 * c:128 * c + 128], SQ)
                last.then_inc(dve_full, 1)

            def queries(g):
                for t in range(2):
                    bank = act_use()
                    for j in range(2):
                        h = GH * g + 2 * t + j
                        for c in range(MC):
                            last = mm(bank[:, 2 * SQ * j:2 * SQ * (j + 1)], wq_sb[:, c, D * h:D * h + D],
                                      xT[:, c, :, :].rearrange("p r q -> p (r q)"), start=(c == 0), stop=(c == MC - 1))
                    last.then_inc(act_full, 1)

            def query_sums():
                pe.wait_ge(act_drained, acts.at(query_uses[-1]))
                bank = dve_use()
                for h in range(GH):
                    for r in range(2):
                        last = mm(bank[0:SQ, 2 * h + r:2 * h + r + 1], q_sq[:, h, SQ * r:SQ * r + SQ], ones_col[:],
                                  start=True, stop=True)
                last.then_inc(dve_full, 1)

            query_uses = []
            pe.wait_ge(consts_ready, 7)
            pe.wait_ge(gatew_loaded, 16)
            bank = dve_use()
            for c in range(MC):
                last = transpose(bank[:, E * c:E * c + E], gwn_sb[:, 128 * c:128 * c + 128], E)
            last.then_inc(dve_full, 1)
            for c in range(CC):
                transpose_ctx(0, 0, c)
            for r in range(2):
                transpose_x(r, r)
            pe.wait_ge(dve_drained, dves.count)
            pe.wait_ge(wq_loaded, 16)
            queries(0)
            query_uses.append(acts.count)
            query_sums()
            queries(1)
            query_uses.append(acts.count)
            pe.wait_ge(wk_split, 2)
            pe.wait_ge(wv_loaded, 16)
            pe.wait_ge(wo_loaded, 16)

            def steps(s, l):
                p = s.pair
                n = UNITS * p + l
                new, mid, old = s.cur, s.unit(l - 1), s.unit(l - 2)
                mid_g, mid_slot = (l - 1) % NG, (l - 1) % UNITS // NG
                old_g, old_slot = (l - 2) % NG, (l - 2) % UNITS // NG
                pT_uses, kT_uses, mix_uses = [], [], []

                def raw_keys(t, c):
                    slot, g = l // NG, l % NG
                    for rows_part, weights_part in ((ctxT_hi, wk_lo), (ctxT_hi, wk_hi), (ctxT_lo, wk_hi)):
                        last = mm(ps_k[:, t, :], rows_part[:, slot, c, 128 * t:128 * t + 128],
                                  weights_part[:, c, GH * D * g:GH * D * (g + 1)],
                                  start=(c == 0 and weights_part is wk_lo),
                                  stop=(c == CC - 1 and rows_part is ctxT_lo))
                    if t == KT - 1 and c == CC - 1:
                        last.then_inc(k_full, 1)

                def transpose_xn2(r):
                    pe.wait_ge(xn2_ready, 2 * p + (1 if r == 0 else 0))
                    bank = dve_use()
                    for c in range(MC):
                        last = transpose(bank[:, SQ * c:SQ * c + SQ], xn2[:, r, 128 * c:128 * c + 128], SQ)
                    last.then_inc(dve_full, 1)

                def gate_logits():
                    bank = dve_use()
                    for c in range(MC):
                        last = mm(bank[0:SQ, 0:E], xn2T[:, c, :], gwT[:, c, :], start=(c == 0), stop=(c == MC - 1))
                    last.then_inc(dve_full, 1)

                def short_uses():
                    if (l == 7 and s.nxt) or (l in (0, 1, 2) and s.cur):
                        yield query_sums
                    for at, rel in ((3, -1), (7, 0)):
                        if l == at and s.batch(rel):
                            yield lambda: transpose_xn2(rel % 2)
                    for at, rel in ((0, -2), (4, -1)):
                        if l == at and s.batch(rel):
                            yield gate_logits
                    for at, r in ((4, 0), (5, 1)):
                        if l == at and s.nxt:
                            yield lambda: transpose_x(r, 2 * p + 2 + r)
                    if (l == 3 and s.cur) or (l == 7 and s.nxt):
                        slot = (l // NG + 1) % 2
                        for c in range(CC):
                            yield lambda: transpose_ctx(slot, p if slot else p + 1, c)
                        ctx_use[0] = dves.count

                def transpose_probs(t):
                    bank = act_use()
                    for h in range(GH):
                        last = transpose(bank[0:KROWS[t], SQ * h:SQ * h + SQ],
                                         probs[:, h, 128 * t:128 * t + KROWS[t]], SQ)
                    last.then_inc(act_full, 1)
                    pT_uses.append(acts.count)

                def transpose_keys(h):
                    bank = act_use()
                    for t in range(KT):
                        last = transpose(bank[:, 128 * t:128 * t + KROWS[t]], kn[0:KROWS[t], t, h, :],
                                         KROWS[t])
                    last.then_inc(act_full, 1)
                    kT_uses.append(acts.count)

                def scores(hp):
                    u = n - 1
                    pe.wait_ge(act_drained, acts.at(kT_uses[2 * hp + 1]))
                    wait_for(pe, exp_done, GH * u + 2 * hp)
                    for j in range(2):
                        h = 2 * hp + j
                        last = mm(ps_s[0:SQ, j, 0:SK], qT[:, GH * mid_g + h, mid_slot, :], kT[:, h, :],
                                  start=True, stop=True)
                    last.then_inc(s_full, 1)

                def mix_context(c):
                    bank = act_use()
                    for t in range(KT):
                        last = mm(bank[:, 0:GH * SQ], ctx_in[0:KROWS[t], old_slot, t, 128 * c:128 * c + 128],
                                  pT[0:KROWS[t], t, :], start=(t == 0), stop=(t == KT - 1))
                    last.then_inc(act_full, 1)
                    mix_uses.append(acts.count)

                if new:
                    if l in (0, 4):
                        pe.wait_ge(dve_drained, dves.at(ctx_use[0]))
                    wait_for(pe, kn_ready, n)
                short = short_uses()
                for i in range(KT * CC):
                    if new:
                        raw_keys(i // CC, i % CC)
                    if mid and i < GH:
                        if i == 0:
                            pe.wait_ge(kn_ready, n)
                        transpose_keys(i)
                    if old and i >= GH:
                        if i == GH:
                            pe.wait_ge(probs_ready, 2 * (n - 2) + 2)
                        transpose_probs(i - GH)
                    if i % 2 == 1:
                        next(short, lambda: None)()
                for use in short:
                    use()
                if old:
                    transpose_probs(KT - 1)
                if mid:
                    scores(0)
                for at, rel in ((2, -1), (6, 0)):
                    if l == at and s.batch(rel):
                        bank = dve_use()
                        for h in range(H):
                            last = mm(bank[0:SQ, :], oT[:, h, :], wo_sb[:, h, :], start=(h == 0), stop=(h == H - 1))
                        last.then_inc(dve_full, 1)
                if old:
                    pe.wait_ge(act_drained, acts.at(pT_uses[-1]))
                    mix_context(0)
                    mix_context(1)
                if (l in (6, 7) and s.nxt) or (l in (0, 1) and s.cur):
                    queries({6: 0, 7: 1, 0: 2, 1: 3}[l])
                    query_uses.append(acts.count)
                if mid:
                    scores(1)
                if old:
                    pe.wait_ge(act_drained, acts.at(mix_uses[-1]))
                    bank = dve_use()
                    for h in range(GH):
                        for c in range(CC):
                            last = mm(bank[:, SQ * h:SQ * h + SQ],
                                      wv_sb[:, c, D * (GH * old_g + h):D * (GH * old_g + h + 1)],
                                      mixT[:, c, SQ * h:SQ * h + SQ], start=(c == 0), stop=(c == CC - 1))
                            if old_g == NG - 1 and h == 0 and c == 0:
                                last.then_inc(ctx_free, 1)
                    last.then_inc(dve_full, 1)

            ctx_use = [dves.count]
            run(pe, steps, [acts, dves])

            pe.wait_ge(picks_done, HOT_SUM_STEP)
            for lhs, dst in ((before, ps_rank), (ones_sq, ps_count)):
                for c in range(0, B * E, 512):
                    w = min(512, B * E - c)
                    last = mm(dst[:, c:c + w], lhs[:], hot_sum[:].rearrange("p b e -> p (b e)")[:, c:c + w],
                              start=True, stop=True)
                last.then_inc(ranks_full, 1)
            for m in range(TOPK * B):
                pe.wait_ge(vals_ready, 2 * m + 2)
                mm(ps_map[:, 0:2 * NT], hot_lo[:, m % NH, :], hot_val[:, m % NH, :, :].rearrange("p a t -> p (a t)"),
                   start=(m == 0), stop=(m == TOPK * B - 1)).then_inc(map_step, 1)

            def transpose_tile(j, i):
                pe.wait_ge(x_gathered[i], 16 // XB * (j - i) + 16)
                wait_for(pe, xT_drained, j)
                for c in range(MC):
                    last = transpose(ps_xT[:, 128 * c:128 * c + 128], x_tile[:, i, 128 * c:128 * c + 128], 128)
                last.then_inc(xT_full, 1)

            wr = w_ring[:].rearrange("p b w -> p (b w)")
            br = b_rows[:].rearrange("s e n -> s (e n)")

            def stage(j, i, has):
                r = i % 2
                if has[0]:
                    e = pe.value_load(tile_tab[0:1, 0, ds(j, 1)], min_val=0, max_val=E - 1)
                    w = pe.value_load(tile_tab[0:1, 1, ds(j, 1)], min_val=0, max_val=(NB - 1) * EW)
                    pe.wait_ge(w_loaded, 48 * e + 48)
                    pe.wait_ge(xT_drained, j + 1)
                    wait_for(pe, gu_drained, j - 1)
                    mm(ps_gu[:, r, :], ones3[:], br[:, ds(e * (2 * F + DM), 2 * F)], start=True, stop=False)
                    for c in range(MC):
                        last = mm(ps_gu[:, r, :], xT_tile[:, r, c, :], wr[:, ds(w + c * 2 * F, 2 * F)],
                                  start=False, stop=(c == MC - 1))
                    last.then_inc(gu_full, 1)
                if has[1]:
                    pe.wait_ge(hid_ready, j)
                    wait_for(pe, hT_drained, j - 1)
                    for c in range(FC):
                        last = transpose(ps_hT[:, 128 * c:128 * c + 128], hid[:, 1 - r, 128 * c:128 * c + 128], 128)
                    last.then_inc(hT_full, 1)
                if has[2]:
                    transpose_tile(j + 1, (i + 1) % XB)
                if has[1]:
                    eb = pe.value_load(tile_tab[0:1, 0, ds(j - 1, 1)], min_val=0, max_val=E - 1)
                    wb = pe.value_load(tile_tab[0:1, 1, ds(j - 1, 1)], min_val=0, max_val=(NB - 1) * EW)
                    pe.wait_ge(hT_drained, j)
                    wait_for(pe, o_drained, j - 2)
                    mm(ps_o[1 - r][:], ones3[:], br[:, ds(eb * (2 * F + DM) + 2 * F, DM)], start=True, stop=False)
                    for c in range(FC):
                        last = mm(ps_o[1 - r][:], hidT[:, 1 - r, c, :], wr[:, ds(wb + MC * 2 * F + c * DM, DM)],
                                  start=False, stop=(c == FC - 1))
                    last.then_inc(o_full, 1)

            pe.wait_ge(table_ready, 1)
            pe.wait_ge(rows_loaded, 16)
            transpose_tile(0, 0)
            expert_tiles(pe, stage)


NAMES = ["x", "ctx_1024", "g_xattn", "g_ffn", "L0_xattn_Wq", "L0_xattn_Wk", "L0_xattn_Wv", "L0_xattn_Wo",
         "L0_xattn_gq", "L0_xattn_gk", "L0_ffn_gate_w", "L0_ffn_gate_b", "L0_ffn_w_gate", "L0_ffn_b_gate",
         "L0_ffn_w_up", "L0_ffn_b_up", "L0_ffn_w_down", "L0_ffn_b_down"]


def kernel(**inputs):
    import numpy as np
    import concourse.bacc as bacc
    from concourse.bass_utils import run_bass_kernel_spmd

    nc = bacc.Bacc("TRN2", target_bir_lowering=False, num_devices=1)
    arrays, args = {}, []
    for name in NAMES:
        a = np.ascontiguousarray(inputs[name])
        arrays[f"in_{name}"] = a
        args.append(nc.dram_tensor(f"in_{name}", a.shape, mybir.dt.from_np(a.dtype), kind="ExternalInput").ap())
    shape = inputs["x"].shape
    args.append(nc.dram_tensor("out", shape, fp32, kind="ExternalOutput").ap())
    flamingo_block(nc, *args)
    r = run_bass_kernel_spmd(nc, [arrays], core_ids=[0])
    return r.results[0]["out"]
```

```python
from contextlib import ExitStack

import concourse.bass as bass
from concourse import mybir
from concourse.bass import ds

fp32 = mybir.dt.float32
f32r = mybir.dt.float32r
bf16 = mybir.dt.bfloat16
i32 = mybir.dt.int32
u32 = mybir.dt.uint32
ALU = mybir.AluOpType
ACT = mybir.ActivationFunctionType
X = mybir.AxisListType.X


class Uses:

    def __init__(self, per_pair, pairs):
        self.per_pair, self.pairs, self.count, self.pair = per_pair, pairs, 0, None

    def take(self):
        self.count += 1
        return self.count

    def at(self, use):
        return use if self.pair is None else use + (self.pair - 1) * self.per_pair

    def enter_loop(self, pair):
        self.pair, self.entered = pair, self.count

    def leave_loop(self):
        assert self.count - self.entered == self.per_pair
        self.count += self.per_pair * (self.pairs - 3)
        self.pair = None


def wait_for(eng, sem, value):
    if not isinstance(value, int) or value > 0:
        eng.wait_ge(sem, value)


def flamingo_block(nc, x, ctx, g_xattn, g_ffn, wq, wk, wv, wo, gq, gk,
                   gate_w, gate_b, w_gate, b_gate, w_up, b_up, w_down, b_down, out):
    B, SQ, DM = x.shape
    SK, DC = ctx.shape[1:]
    D = gq.shape[0]
    H = wq.shape[1] // D
    E, _, F = w_gate.shape
    TOPK = 4
    EPS = 1e-5
    PAIRS = B // 2
    GH = 4
    NG = H // GH
    UNITS = 2 * NG
    MC, CC = DM // 128, DC // 128
    KT = -(-SK // 128)
    KROWS = [min(128, SK - 128 * t) for t in range(KT)]
    ctxstack = ExitStack()
    with ctxstack as outer:
        def sem(name):
            return outer.enter_context(nc.semaphore(name))

        def keep(name, shape, dt=fp32):
            return outer.enter_context(nc.sbuf_tensor(name, shape, dt))

        bias_dram = nc.dram_tensor("bias_parts", (E, 3, 2 * F + DM), bf16, kind="Internal").ap()
        xn2_dram = nc.dram_tensor("xn2_rows", (B * SQ, DM), fp32, kind="Internal").ap()

        ident = keep("ident", [128, 128])
        minus_half = keep("minus_half", [128, 16])
        minus_one = keep("minus_one", [128, 4])
        tanh_x = keep("tanh_x", [128, 1])
        tanh_f = keep("tanh_f", [128, 1])
        best = keep("best", [SQ, 8])
        best_index = keep("best_index", [SQ, 8], u32)
        top_value = keep("top_value", [SQ, B, TOPK])
        top_index = keep("top_index", [SQ, B, TOPK], u32)

        attn = ExitStack()

        def sb(name, shape, dt=fp32):
            return attn.enter_context(nc.sbuf_tensor(name, shape, dt))

        wq_sb = sb("wq_sb", [128, MC, H * D])
        whole = ExitStack()
        wk_whole = whole.enter_context(nc.sbuf_tensor("wk_whole", [128, CC, H * D], fp32))
        ctx_whole = whole.enter_context(nc.sbuf_tensor("ctx_whole", [128, 2, KT, DC], fp32))
        pT_whole = whole.enter_context(nc.sbuf_tensor("pT_whole", [128, KT, GH * SQ], fp32))
        whole.close()
        wk_lo = sb("wk_lo", [128, CC, H * D], f32r)
        ctx_lo = sb("ctx_lo", [128, 2, KT, DC], f32r)
        pT_lo = sb("pT_lo", [128, KT, GH * SQ], f32r)
        ctx_hi = sb("ctx_hi", [128, 2, KT, DC], f32r)
        pT_hi = sb("pT_hi", [128, KT, GH * SQ], f32r)
        wk_hi = sb("wk_hi", [128, CC, H * D], f32r)
        wv_sb = sb("wv_sb", [128, CC, H * D])
        wo_sb = sb("wo_sb", [128, H, DM])
        gwT = sb("gwT", [128, MC, E])
        gate_bias = sb("gate_bias", [SQ, E])
        gq_col = sb("gq_col", [D, 1])
        gk_col = sb("gk_col", [D, 1])
        gqk = sb("gqk", [D, 1])
        gx_row = sb("gx_row", [128, 2])
        ones_col = sb("ones_col", [128, 1])
        x_in = sb("x_in", [SQ, 2, DM])
        xT = sb("xT", [128, MC, 2, SQ])
        ln_stats = sb("ln_stats", [SQ, 2, 2, 6])
        ln_mv = sb("ln_mv", [SQ, 2, 2, 2])
        ln_var = sb("ln_var", [SQ, 2, 2, 1])
        ln_rstd = sb("ln_rstd", [SQ, 2, 2, 1])
        ctxT_hi = sb("ctxT_hi", [128, 2, CC, KT * 128], f32r)
        ctxT_lo = sb("ctxT_lo", [128, 2, CC, KT * 128], f32r)
        qT = sb("qT", [128, H, 2, SQ])
        q_sq = sb("q_sq", [128, GH, 2 * SQ])
        q_ss = sb("q_ss", [SQ, GH * 2])
        q_se = sb("q_se", [SQ, GH * 2])
        rq = sb("rq", [SQ, NG, GH, 2])
        k_ss = sb("k_ss", [128, KT, GH])
        k_se = sb("k_se", [128, KT, GH])
        rk = sb("rk", [128, KT, GH])
        kn = sb("kn", [128, KT, GH, D])
        kT = sb("kT", [128, GH, SK])
        s_max = sb("s_max", [SQ, 2, 2])
        s_bias = sb("s_bias", [SQ, 2, 2])
        probs = sb("probs", [SQ, GH, SK])
        gwn_sb = probs[0:E, :, :].rearrange("p h k -> p (h k)")[:, 0:DM]
        p_sum = sb("p_sum", [SQ, GH])
        p_inv = sb("p_inv", [SQ, GH])
        mixT = sb("mixT", [128, CC, GH * SQ])
        oT = sb("oT", [128, H, SQ])
        x1 = sb("x1", [SQ, 2, DM])
        xn2 = sb("xn2", [SQ, 2, DM])
        xn2T = sb("xn2T", [128, MC, SQ])
        logits = sb("logits", [SQ, 2, E])
        attn.close()

        NT = -(-(B * SQ * TOPK + E * 127) // 128)
        XB = 4
        NT += -NT % XB
        NB = 4
        EW = MC * 2 * F + (F // 128) * DM
        FC = F // 128
        moe = ExitStack()

        def sm(name, shape, dt=fp32):
            return moe.enter_context(nc.sbuf_tensor(name, shape, dt))

        w_ring = sm("w_ring", [128, NB, EW])
        b_rows = sm("b_rows", [3, E, 2 * F + DM], bf16)
        ones3 = sm("ones3", [3, 128], bf16)
        t_end_i = sm("t_end_i", [SQ, E], i32)
        tile_tab = sm("tile_tab", [1, 2, NT], i32)
        slot_w = sm("slot_w", [128, NT])
        gather_i = sm("gather_i", [128, NT], u32)
        scatter_i = sm("scatter_i", [128, NT], u32)
        gather_now = sm("gather_now", [128, XB, 1], u32)
        scatter_now = sm("scatter_now", [128, 2, 1], u32)
        routing, tiles = ExitStack(), ExitStack()

        def sr(name, shape, dt=fp32):
            return routing.enter_context(nc.sbuf_tensor(name, shape, dt))

        b_nat = sr("b_nat", [E, 2 * F + DM])
        b_rest = sr("b_rest", [E, 2 * F + DM])
        b_part = sr("b_part", [E, 3, 2 * F + DM], bf16)
        iota_e_i = sr("iota_e_i", [128, E], i32)
        iota_e = sr("iota_e", [128, E])
        iota_l_i = sr("iota_l_i", [128, 128], i32)
        iota_l = sr("iota_l", [128, 128])
        iota_t_i = sr("iota_t_i", [128, NT], i32)
        iota_t = sr("iota_t", [128, NT])
        token_i = sr("token_i", [128, B], i32)
        token_1 = sr("token_1", [128, B])
        before = sr("before", [SQ, SQ])
        ones_sq = sr("ones_sq", [SQ, SQ])
        ones_eb = sr("ones_eb", [SQ, E, B])
        chosen = sr("chosen", [SQ, B, TOPK])
        v_gap = sr("v_gap", [SQ, B, TOPK])
        v_exp = sr("v_exp", [SQ, B, TOPK])
        v_sum = sr("v_sum", [SQ, B, 1])
        v_inv = sr("v_inv", [SQ, B, 1])
        weight = sr("weight", [SQ, B, TOPK])
        hot = sr("hot", [SQ, TOPK, B, E])
        hot_sum = sr("hot_sum", [SQ, B, E])
        count = sr("count", [SQ, E, B])
        run_sum = sr("run_sum", [SQ, E, B])
        n_e = sr("n_e", [SQ, E])
        n_e_i = sr("n_e_i", [SQ, E], i32)
        n_t_i = sr("n_t_i", [SQ, E], i32)
        n_t = sr("n_t", [SQ, E])
        t_end = sr("t_end", [SQ, E])
        shift = sr("shift", [SQ, E])
        place = sr("place", [SQ, B, E])
        wide = sr("wide", [SQ, max(TOPK * B, NT) * E])
        hot_place = wide[:, 0:TOPK * B * E].rearrange("p (k b e) -> p k b e", k=TOPK, b=B)
        tile_cmp = wide[0:1, 0:NT * E].rearrange("p (t e) -> p t e", e=E)
        slot_f = sr("slot_f", [SQ, TOPK, B])
        slot_i = sr("slot_i", [SQ, TOPK, B], i32)
        slot_hi_i = sr("slot_hi_i", [SQ, TOPK, B], i32)
        slot_lo_i = sr("slot_lo_i", [SQ, TOPK, B], i32)
        slot_hi = sr("slot_hi", [SQ, TOPK, B])
        slot_lo = sr("slot_lo", [SQ, TOPK, B])
        NH = 3
        hot_lo = sr("hot_lo", [SQ, NH, 128], f32r)
        hot_hi = sr("hot_hi", [SQ, NH, NT])
        hot_val = sr("hot_val", [SQ, NH, 3, NT], f32r)
        weight_hi = sr("weight_hi", [SQ, B, TOPK], f32r)
        weight_lo = sr("weight_lo", [SQ, B, TOPK])
        tile_e = sr("tile_e", [1, NT])
        tile_b = sr("tile_b", [1, NT], i32)
        tile_b_f = sr("tile_b_f", [1, NT])
        slot_tok = sr("slot_tok", [128, NT])
        pad_far = sr("pad_far", [128, NT])
        routing.close()

        def st(name, shape, dt=fp32):
            return tiles.enter_context(nc.sbuf_tensor(name, shape, dt))

        x_tile = st("x_tile", [128, XB, DM])
        xT_tile = st("xT_tile", [128, 2, MC, 128])
        g_min = st("g_min", [128, 2, F])
        u_min = st("u_min", [128, 2, F])
        sig = st("sig", [128, 2, F])
        glu = st("glu", [128, 2, F])
        hid = st("hid", [128, 2, F])
        hidT = st("hidT", [128, 2, FC, 128])
        o_tile = st("o_tile", [128, 2, DM])
        tiles.close()
        moe.close()

        def ps(name, shape):
            return outer.enter_context(nc.psum_tensor(name, shape, fp32))

        ps_k = ps("ps_k", [128, KT, 512])
        ps_act0 = ps("ps_act0", [128, 512])
        ps_s = ps("ps_s", [128, 2, 512])
        ps_act1 = ps("ps_act1", [128, 512])
        ps_dve = ps("ps_dve", [128, 512])
        act_bank = [ps_act0, ps_act1]
        HOT_SUM_STEP = 2 + TOPK + TOPK - 1
        ps_rank = ps_k[0:SQ, 0:2, :].rearrange("p a c -> p (a c)")[:, 0:B * E]
        ps_count = ps_s[0:SQ, :, :].rearrange("p a c -> p (a c)")[:, 0:B * E]
        ps_map = ps_dve
        ps_xT, ps_hT, ps_gu, ps_o = ps_act0, ps_act1, ps_s, [ps_dve, ps_k[:, 0, :]]

        ctx_loaded = [sem(f"ctx_loaded{r}") for r in range(2)]
        x_loaded = [sem(f"x_loaded{r}") for r in range(2)]
        xres_loaded = [sem(f"xres_loaded{r}") for r in range(2)]
        wk_loaded, wq_loaded, wv_loaded, wo_loaded = (sem(f"w{c}_loaded") for c in "kqvo")
        wk_split = sem("wk_split")
        ctxT_rounded = sem("ctxT_rounded")
        ctx_split = sem("ctx_split")
        pT_rounded = sem("pT_rounded")
        pT_split = sem("pT_split")
        wq0_loaded = sem("wq0_loaded")
        small_loaded = sem("small_loaded")
        gatew_loaded = sem("gatew_loaded")
        consts_ready = sem("consts_ready")
        scalars_ready = sem("scalars_ready")
        ctx_free = sem("ctx_free")
        k_full = sem("k_full")
        ksq_ready = sem("ksq_ready")
        kss_ready = sem("kss_ready")
        kse_ready = sem("kse_ready")
        rk_ready = sem("rk_ready")
        kn_ready = sem("kn_ready")
        act_full = sem("act_full")
        act_drained = sem("act_drained")
        dve_full = sem("dve_full")
        dve_drained = sem("dve_drained")
        qse_ready = sem("qse_ready")
        rq_ready = sem("rq_ready")
        s_full = sem("s_full")
        smax_ready = sem("smax_ready")
        sbias_ready = sem("sbias_ready")
        exp_done = sem("exp_done")
        pinv_ready = sem("pinv_ready")
        probs_ready = sem("probs_ready")
        bn_ready = [sem(f"bn_ready{k}") for k in (1, 2)]
        mv_ready = [sem(f"mv_ready{k}") for k in (1, 2)]
        var_ready = [sem(f"var_ready{k}") for k in (1, 2)]
        rstd_ready = [sem(f"rstd_ready{k}") for k in (1, 2)]
        xn_ready = sem("xn_ready")
        xn2_ready = sem("xn2_ready")
        x1_stored = [sem(f"x1_stored{r}") for r in range(2)]
        xn2_stored = [sem(f"xn2_stored{r}") for r in range(2)]
        logits_ready = sem("logits_ready")
        best_ready = sem("best_ready")
        top_ready = sem("top_ready")

        picks_done = sem("picks_done")
        gaps_exp = sem("gaps_exp")
        ranks_full = sem("ranks_full")
        hots_ready = sem("hots_ready")
        vals_ready = sem("vals_ready")
        map_step = sem("map_step")
        moe_consts = sem("moe_consts")
        moe_floats = sem("moe_floats")
        bias_step = sem("bias_step")
        bias_loaded = sem("bias_loaded")
        bias_stored = sem("bias_stored")
        rows_loaded = sem("rows_loaded")
        table_ready = sem("table_ready")
        w_loaded = sem("w_loaded")
        idx_copied = sem("idx_copied")
        sidx_copied = sem("sidx_copied")
        x_gathered = [sem(f"x_gathered{r}") for r in range(XB)]
        xT_full = sem("xT_full")
        xT_drained = sem("xT_drained")
        gu_full = sem("gu_full")
        g_ready = sem("g_ready")
        gu_drained = sem("gu_drained")
        sig_ready = sem("sig_ready")
        glu_ready = sem("glu_ready")
        hid_ready = sem("hid_ready")
        hT_full = sem("hT_full")
        hT_drained = sem("hT_drained")
        o_full = sem("o_full")
        o_drained = sem("o_drained")
        pool_turns = sem("pool_turns")
        dve_turns = sem("dve_turns")
        sp_turns = sem("sp_turns")
        added = sem("added")

        ACT_USES = UNITS * (GH + KT + CC) + 2 * NG
        DVE_USES = UNITS + 2 * 3 + NG + 2 * CC + 2

        class Span:

            def __init__(self, place, pair, prev, cur, nxt):
                self.place, self.pair, self.prev, self.cur, self.nxt = place, pair, prev, cur, nxt

            def unit(self, k):
                return self.prev if k < 0 else self.cur

            def batch(self, r):
                return self.prev if r < 0 else (self.cur if r < 2 else self.nxt)

        parts = [(slice(0, 128), slice(0, KT - 1)), (slice(0, KROWS[-1]), slice(KT - 1, KT))]
        probs_use = {}

        def run(eng, steps, uses=()):
            for l in range(UNITS):
                steps(Span("first", 0, False, True, True), l)
            with eng.Fori(1, PAIRS - 1) as pair:
                for u in uses:
                    u.enter_loop(pair)
                for l in range(UNITS):
                    steps(Span("loop", pair, True, True, True), l)
            for u in uses:
                u.leave_loop()
            for l in range(UNITS):
                steps(Span("last", PAIRS - 1, True, True, False), l)
            for l in range(NG + 2):
                steps(Span("after", PAIRS, True, False, False), l)

        def rows(dram, batch):
            return dram[ds(batch, 1), :, :].rearrange("o s d -> (o s) d")

        def ctx_rows_in(eng, batch, slot):
            full = SK // 128
            src = rows(ctx, batch)
            eng.dma_start(ctx_whole[:, slot, 0:full, :],
                          src[0:full * 128, :].rearrange("(t p) c -> p t c", p=128)).then_inc(ctx_loaded[slot], 16)
            eng.dma_start(ctx_whole[0:KROWS[-1], slot, full, :], src[full * 128:SK, :]).then_inc(ctx_loaded[slot], 16)

        def attention_stored(eng):
            for r in range(2):
                eng.wait_ge(x1_stored[r], 16 * PAIRS)
                eng.wait_ge(xn2_stored[r], 16 * PAIRS)

        block = outer.enter_context(nc.Block())

        def expert_tiles(eng, stage):
            stage(0, 0, (True, False, True))
            for j in range(1, XB):
                stage(j, j, (True, True, True))
            with eng.Fori(1, NT // XB - 1) as q:
                for i in range(XB):
                    stage(XB * q + i, i, (True, True, True))
            for i in range(XB):
                stage(NT - XB + i, i, (True, True, i < XB - 1))
            stage(NT, 0, (False, True, False))

        @block.sync
        def _(sp):
            ctx_rows_in(sp, 0, 0)
            for r in range(2):
                sp.dma_start(x_in[:, r, :], rows(x, r)).then_inc(x_loaded[r], 16)
            sp.wait_ge(small_loaded, 16 * 5)
            sp.wait_ge(gatew_loaded, 16)
            for r in range(2):
                sp.wait_ge(x_loaded[r], 16)
            wq_rows = wq.rearrange("(c p) n -> p c n", p=128)
            sp.dma_start(wq_sb[:, :, 0:GH * D], wq_rows[:, :, 0:GH * D]).then_inc(wq0_loaded, 16)
            sp.dma_start(wk_whole[:], wk.rearrange("(c p) n -> p c n", p=128)).then_inc(wk_loaded, 16)
            sp.wait_ge(wk_loaded, 16)
            sp.dma_start(wq_sb[:, :, GH * D:], wq_rows[:, :, GH * D:]).then_inc(wq_loaded, 16)
            sp.dma_start(wv_sb[:], wv.rearrange("(c p) n -> p c n", p=128)).then_inc(wv_loaded, 16)
            sp.dma_start(wo_sb[:], wo.rearrange("(h p) n -> p h n", p=128)).then_inc(wo_loaded, 16)

            def residual_rows_in(p, r):
                wait_for(sp, x1_stored[r], 16 * p)
                wait_for(sp, xn2_stored[r], 16 * p)
                sp.dma_start(x1[:, r, :], rows(x, 2 * p + r)).then_inc(xres_loaded[r], 16)

            def steps(s, l):
                p = s.pair
                if l == 1:
                    if s.cur:
                        residual_rows_in(p, 0)
                    if s.nxt:
                        sp.wait_ge(qse_ready, NG * p + 1)
                        for r in range(2):
                            sp.dma_start(x_in[:, r, :], rows(x, 2 * p + 2 + r)).then_inc(x_loaded[r], 16)
                if l == 5 and s.cur:
                    residual_rows_in(p, 1)
                if l == 2 and s.cur:
                    wait_for(sp, ctx_free, 2 * p)
                    ctx_rows_in(sp, 2 * p + 1, 1)
                if l == 6 and s.nxt:
                    wait_for(sp, ctx_free, 2 * p + 1)
                    ctx_rows_in(sp, 2 * p + 2, 0)
                for at, rel in ((3, -1), (7, 0)):
                    if l == at and s.batch(rel):
                        sp.wait_ge(bn_ready[1], 2 * p + rel + 1)
                        sp.dma_start(rows(out, 2 * p + rel), x1[:, rel % 2, :]).then_inc(x1_stored[rel % 2], 16)
                for at, rel in ((4, -1), (0, -2)):
                    if l == at and s.batch(rel):
                        sp.wait_ge(xn2_ready, 2 * p + rel + 1)
                        sp.dma_start(xn2_dram[ds((2 * p + rel) * SQ, SQ), :], xn2[:, rel % 2, :])\
                          .then_inc(xn2_stored[rel % 2], 16)

            run(sp, steps)
            sp.wait_ge(top_ready, 2 * B)
            attention_stored(sp)
            for part, src in ((slice(0, F), b_gate), (slice(F, 2 * F), b_up), (slice(2 * F, 2 * F + DM), b_down)):
                sp.dma_start(b_nat[:, part], src).then_inc(bias_loaded, 16)

            def load_expert(e, buf):
                gu = w_ring[:, buf, 0:MC * 2 * F].rearrange("p (c n) -> p c n", c=MC)
                sp.dma_start(gu[:, :, 0:F], w_gate[ds(e, 1), :, :].rearrange("o (c p) n -> p (o c) n", p=128))\
                  .then_inc(w_loaded, 16)
                sp.dma_start(gu[:, :, F:2 * F], w_up[ds(e, 1), :, :].rearrange("o (c p) n -> p (o c) n", p=128))\
                  .then_inc(w_loaded, 16)
                sp.dma_start(w_ring[:, buf, MC * 2 * F:EW].rearrange("p (c n) -> p c n", c=FC),
                             w_down[ds(e, 1), :, :].rearrange("o (c p) n -> p (o c) n", p=128)).then_inc(w_loaded, 16)
                sp.wait_ge(w_loaded, 48 * (e + 1))
                sp.sem_inc(sp_turns, 1)

            for e in range(NB):
                load_expert(e, e)
                if e == 0:
                    sp.wait_ge(bias_step, 5)
                    sp.dma_start(bias_dram, b_part[:]).then_inc(bias_stored, 16)
                    sp.wait_ge(bias_stored, 16)
                    sp.dma_start(b_rows[:], bias_dram.rearrange("e s n -> s e n")).then_inc(rows_loaded, 16)
            sp.sem_inc(o_full, 1)
            sp.wait_ge(table_ready, 1)
            with sp.Fori(1, E // NB) as q:
                for j in range(NB):
                    done = sp.value_load(t_end_i[0:1, ds(q * NB + (j - NB), 1)], min_val=1, max_val=NT + 1)
                    sp.wait_ge(o_full, done)
                    load_expert(q * NB + j, j)
            sp.wait_ge(added, 16 * NT)

        @block.gpsimd
        def _(pool):
            pool.dma_start(gq_col[:], gq.rearrange("(p o) -> p o", o=1)).then_inc(small_loaded, 16)
            pool.dma_start(gk_col[:], gk.rearrange("(p o) -> p o", o=1)).then_inc(small_loaded, 16)
            pool.dma_start(gx_row[:, 0:1], g_xattn.partition_broadcast(128)).then_inc(small_loaded, 16)
            pool.dma_start(gx_row[:, 1:2], g_ffn.partition_broadcast(128)).then_inc(small_loaded, 16)
            pool.dma_start(gate_bias[:], gate_b.partition_broadcast(SQ)).then_inc(small_loaded, 16)
            pool.dma_start(gwn_sb, gate_w).then_inc(gatew_loaded, 16)
            pool.memset(ident[:], 0.0).then_inc(consts_ready, 1)
            pool.memset(minus_half[:], -0.5).then_inc(consts_ready, 1)
            pool.memset(minus_one[:], -1.0).then_inc(consts_ready, 1)
            pool.memset(ones_col[:], 1.0).then_inc(consts_ready, 1)
            pool.memset(ctxT_hi[:, :, :, SK:].bitcast(i32), 0).then_inc(consts_ready, 1)
            pool.memset(ctxT_lo[:, :, :, SK:].bitcast(i32), 0).then_inc(consts_ready, 1)
            pool.wait_ge(consts_ready, 6)
            pool.affine_select(out=ident[:], in_=ident[:], compare_op=ALU.not_equal, fill=1.0, base=0,
                               pattern=[[-1, 128]], channel_multiplier=1).then_inc(consts_ready, 1)

            def norm_root(kind, batch, r):
                pool.wait_ge(mv_ready[kind], batch + 1)
                pool.sem_inc(pool_turns, 1)
                pool.tensor_scalar(ln_var[:, kind, r, :], ln_mv[:, kind, r, 1:2], EPS, None, ALU.add)\
                    .then_inc(var_ready[kind], 1)
                pool.wait_ge(var_ready[kind], batch + 1)
                pool.tensor_tensor(ln_rstd[:, kind, r, :], ln_var[:, kind, r, :], minus_half[0:SQ, 0:1], ALU.pow)\
                    .then_inc(rstd_ready[kind], 1)

            def query_root(n, g):
                pool.wait_ge(qse_ready, n)
                pool.tensor_tensor(rq[:, g, :, :].rearrange("p h r -> p (h r)"), q_se[:],
                                   minus_half[0:SQ, 0:2 * GH], ALU.pow).then_inc(rq_ready, 1)

            def split_ctx(slot, batch):
                pool.wait_ge(ctxT_rounded, CC * (batch + 1))
                pool.sem_inc(pool_turns, 1)
                for rows_, ts in parts:
                    pool.tensor_copy(ctx_hi[rows_, slot, ts, :], ctx_whole[rows_, slot, ts, :]).then_inc(ctx_split, 1)
                pool.wait_ge(ctx_split, 4 * batch + 2)
                pool.sem_inc(pool_turns, 1)
                for rows_, ts in parts:
                    pool.tensor_tensor(ctx_lo[rows_, slot, ts, :], ctx_whole[rows_, slot, ts, :],
                                       ctx_hi[rows_, slot, ts, :].bitcast(fp32), ALU.subtract).then_inc(ctx_split, 1)

            for r in range(2):
                norm_root(0, r, r)
            query_root(1, 0)

            def steps(s, l):
                p = s.pair
                n = UNITS * p + l
                def normalise_probs(hp, u):
                    pool.wait_ge(exp_done, GH * u + 2 * hp + 2)
                    pool.tensor_tensor(p_inv[:, 2 * hp:2 * hp + 2], p_sum[:, 2 * hp:2 * hp + 2],
                                       minus_one[0:SQ, 0:2], ALU.pow).then_inc(pinv_ready, 1)
                    pool.wait_ge(pinv_ready, 2 * u + hp + 1)
                    pr = probs[:, 2 * hp:2 * hp + 2, :]
                    pool.tensor_tensor(pr, pr, p_inv[:, 2 * hp:2 * hp + 2].unsqueeze(2)
                                       .broadcast_to([SQ, 2, SK]), ALU.mult).then_inc(probs_ready, 1)

                if s.unit(l - 2):
                    normalise_probs(1, n - 2)
                if s.cur:
                    pool.wait_ge(kss_ready, n + 1)
                    pool.sem_inc(pool_turns, 1)
                    pool.tensor_scalar(k_se[:], k_ss[:], D * EPS, None, ALU.add).then_inc(kse_ready, 1)
                    pool.wait_ge(kse_ready, n + 1)
                    pool.tensor_tensor(rk[:].rearrange("p t h -> p (t h)"), k_se[:].rearrange("p t h -> p (t h)"),
                                       minus_half[:, 0:KT * GH], ALU.pow).then_inc(rk_ready, 1)
                if l == 7 and s.nxt:
                    query_root(NG * p + 5, 0)
                if l in (0, 1, 2) and s.cur:
                    query_root(NG * p + l + 2, l + 1)
                for at, r in ((2, 0), (3, 1)):
                    if l == at and s.nxt:
                        norm_root(0, 2 * p + 2 + r, r)
                if s.unit(l - 1):
                    normalise_probs(0, n - 1)
                for at, rel in ((3, -1), (7, 0)):
                    if l == at and s.batch(rel):
                        norm_root(1, 2 * p + rel, rel % 2)
                for at, rel in ((1, 0), (5, 1)):
                    if l == at and s.cur:
                        split_ctx(rel, 2 * p + rel)

            run(pool, steps)

            pool.wait_ge(top_ready, 2 * B)
            attention_stored(pool)
            pool.iota(iota_e_i[:], pattern=[[1, E]], base=0, channel_multiplier=0).then_inc(moe_consts, 1)
            pool.iota(iota_l_i[:], pattern=[[1, 128]], base=0, channel_multiplier=0).then_inc(moe_consts, 1)
            pool.iota(iota_t_i[:], pattern=[[1, NT]], base=0, channel_multiplier=0).then_inc(moe_consts, 1)
            pool.iota(token_i[:], pattern=[[SQ, B]], base=1, channel_multiplier=1).then_inc(moe_consts, 1)
            pool.memset(before[:], 1.0).then_inc(moe_consts, 1)
            pool.memset(ones_sq[:], 1.0).then_inc(moe_consts, 1)
            pool.memset(ones_eb[:], 1.0).then_inc(moe_consts, 1)
            pool.memset(ones3[:], 1.0).then_inc(moe_consts, 1)
            pool.wait_ge(moe_consts, 8)
            pool.affine_select(out=before[:], in_=before[:], compare_op=ALU.is_gt, fill=0.0, base=0,
                               pattern=[[1, SQ]], channel_multiplier=-1).then_inc(moe_consts, 1)
            pool.wait_ge(bias_loaded, 48)
            pool.tensor_copy(b_part[:, 0, :], b_nat[:]).then_inc(bias_step, 1)
            pool.wait_ge(bias_step, 1)
            pool.tensor_tensor(b_rest[:], b_nat[:], b_part[:, 0, :], ALU.subtract).then_inc(bias_step, 1)
            pool.wait_ge(bias_step, 2)
            pool.tensor_copy(b_part[:, 1, :], b_rest[:]).then_inc(bias_step, 1)
            pool.wait_ge(bias_step, 3)
            pool.tensor_tensor(b_rest[:], b_rest[:], b_part[:, 1, :], ALU.subtract).then_inc(bias_step, 1)
            pool.wait_ge(bias_step, 4)
            pool.tensor_copy(b_part[:, 2, :], b_rest[:]).then_inc(bias_step, 1)

            pool.wait_ge(table_ready, 1)

            def gather(j, i):
                wait_for(pool, xT_full, j - XB + 1)
                pool.tensor_copy(gather_now[:, i, :], gather_i[:, ds(j, 1)]).then_inc(idx_copied, 1)
                pool.wait_ge(idx_copied, j + 1)
                pool.sem_inc(pool_turns, 1)
                pool.indirect_dma_start(out=x_tile[:, i, :], out_offset=None, in_=xn2_dram,
                                        in_offset=bass.IndirectOffsetOnAxis(ap=gather_now[:, i, :], axis=0))\
                    .then_inc(x_gathered[i], 16)

            def add_rows(j, i):
                pool.tensor_copy(scatter_now[:, i % 2, :], scatter_i[:, ds(j, 1)]).then_inc(sidx_copied, 1)
                pool.wait_ge(sidx_copied, j + 1)
                pool.wait_ge(o_drained, j + 1)
                wait_for(pool, added, 16 * j)
                pool.sem_inc(pool_turns, 1)
                pool.indirect_dma_start(out=out.rearrange("b s d -> (b s) d"),
                                        out_offset=bass.IndirectOffsetOnAxis(ap=scatter_now[:, i % 2, :], axis=0),
                                        in_=o_tile[:, i % 2, :], in_offset=None, bounds_check=B * SQ - 1,
                                        oob_is_err=False, compute_op=ALU.add).then_inc(added, 16)

            AHEAD = 5
            for j in range(AHEAD):
                gather(j, j % XB)
            for j in range(XB):
                add_rows(j, j)
                gather(j + AHEAD, (j + AHEAD) % XB)
            with pool.Fori(1, (NT - AHEAD) // XB) as q:
                for i in range(XB):
                    add_rows(XB * q + i, i)
                    gather(XB * q + i + AHEAD, (i + AHEAD) % XB)
            for j in range((NT - AHEAD) // XB * XB, NT):
                add_rows(j, j % XB)
                if j + AHEAD < NT:
                    gather(j + AHEAD, (j + AHEAD) % XB)
            pool.wait_ge(added, 16 * NT)

        @block.scalar
        def _(act):
            act.wait_ge(small_loaded, 16 * 5)
            act.activation(tanh_x[:], gx_row[:, 0:1], ACT.Tanh).then_inc(scalars_ready, 1)
            act.activation(tanh_f[:], gx_row[:, 1:2], ACT.Tanh).then_inc(scalars_ready, 1)
            act.wait_ge(scalars_ready, 4)
            uses = Uses(ACT_USES, PAIRS)

            def drain(dst, src, width, scale=None):
                u = uses.take()
                act.wait_ge(act_full, uses.at(u))
                bank = act_bank[u % 2]
                act.activation(dst, src(bank), ACT.Copy, **({} if scale is None else {"scale": scale}))\
                   .then_inc(act_drained, 1)

            def drain_queries(g, t):
                u = uses.take()
                act.wait_ge(act_full, uses.at(u))
                bank = act_bank[u % 2]
                h = GH * g + 2 * t
                act.activation(qT[:, h:h + 2, :, :].rearrange("p h r q -> p (h r q)"), bank[:, 0:4 * SQ], ACT.Copy,
                               scale=gqk[:, 0:1])
                act.activation(q_sq[:, 2 * t:2 * t + 2, :].rearrange("p h q -> p (h q)"), bank[:, 0:4 * SQ],
                               ACT.Square).then_inc(act_drained, 1)

            for g in range(2):
                for t in range(2):
                    drain_queries(g, t)

            def steps(s, l):
                p = s.pair
                n = UNITS * p + l
                def drain_probs(t):
                    drain(pT_whole[0:KROWS[t], t, :], lambda bank: bank[0:KROWS[t], 0:GH * SQ], GH * SQ)

                def drain_keys(h):
                    drain(kT[:, h, :], lambda bank: bank[:, 0:SK], SK)

                def drain_mix(c):
                    drain(mixT[:, c, :], lambda bank: bank[:, 0:GH * SQ], GH * SQ)

                def exponentials(hp, lag):
                    u, g, r = n - lag, (l - lag) % NG, (l - lag) % UNITS // NG
                    act.wait_ge(sbias_ready, 2 * u + hp + 1)
                    for j in range(2):
                        h = 2 * hp + j
                        act.activation(probs[:, h, :], ps_s[0:SQ, j, 0:SK], ACT.Exp,
                                       bias=s_bias[:, hp, j:j + 1], scale=rq[:, g, h, r:r + 1],
                                       accum_out=p_sum[:, h:h + 1]).then_inc(exp_done, 1)

                if s.unit(l - 1):
                    for h in range(GH // 2):
                        drain_keys(h)
                if s.unit(l - 2):
                    exponentials(1, 2)
                if s.unit(l - 1):
                    for h in range(GH // 2, GH):
                        drain_keys(h)
                if s.cur:
                    act.wait_ge(k_full, n + 1)
                    act.activation(kn[:].rearrange("p t h d -> p (t h d)"),
                                   ps_k[:].rearrange("p t c -> p (t c)"), ACT.Square).then_inc(ksq_ready, 1)
                if s.unit(l - 3):
                    for c in range(CC):
                        drain_mix(c)
                if s.unit(l - 2):
                    for t in range(KT):
                        drain_probs(t)
                    probs_use[s.place, l] = uses.count
                if s.unit(l - 1):
                    exponentials(0, 1)
                if (l in (6, 7) and s.nxt) or (l in (0, 1) and s.cur):
                    for t in range(2):
                        drain_queries({6: 0, 7: 1, 0: 2, 1: 3}[l], t)

            run(act, steps, [uses])

            act.wait_ge(picks_done, 2)
            act.activation(v_exp[:], v_gap[:], ACT.Exp).then_inc(gaps_exp, 1)

            def values(m, j):
                k, b = m // B, m % B
                act.wait_ge(hots_ready, 3 * m + 3)
                wait_for(act, map_step, m - NH + 1)
                for part, scale in ((1, weight_hi[:, b, k:k + 1].bitcast(fp32)), (2, weight_lo[:, b, k:k + 1])):
                    act.activation(hot_val[:, j, part, :], hot_hi[:, j, :], ACT.Copy, scale=scale)\
                       .then_inc(vals_ready, 1)

            for m in range(TOPK * B):
                values(m, m % NH)

            act.wait_ge(table_ready, 1)

            def stage(j, i, has):
                r = i % 2
                if has[1]:
                    act.wait_ge(hT_full, j)
                    act.activation(hidT[:, 1 - r, :, :].rearrange("p c n -> p (c n)"), ps_hT[:, 0:F], ACT.Copy)\
                       .then_inc(hT_drained, 1)
                if has[2]:
                    act.wait_ge(xT_full, j + 2)
                    act.activation(xT_tile[:, 1 - r, :, :].rearrange("p c n -> p (c n)"), ps_xT[:, 0:DM], ACT.Copy)\
                       .then_inc(xT_drained, 1)
                if has[0]:
                    act.wait_ge(g_ready, j + 1)
                    act.activation(sig[:, r, :], g_min[:, r, :], ACT.Sigmoid, scale=1.702).then_inc(sig_ready, 1)
                if has[1]:
                    act.wait_ge(o_full, j + 1)
                    wait_for(act, added, 16 * (j - 2))
                    act.activation(o_tile[:, 1 - r, :], ps_o[1 - r][:], ACT.Copy, scale=slot_w[:, ds(j - 1, 1)])\
                       .then_inc(o_drained, 1)

            act.wait_ge(xT_full, 1)
            act.activation(xT_tile[:, 0, :, :].rearrange("p c n -> p (c n)"), ps_xT[:, 0:DM], ACT.Copy)\
               .then_inc(xT_drained, 1)
            expert_tiles(act, stage)

        @block.vector
        def _(dve):
            dve.wait_ge(small_loaded, 16 * 5)
            dve.tensor_scalar(gqk[:], gq_col[:], gk_col[:, 0:1], None, ALU.mult).then_inc(scalars_ready, 1)
            dve.wait_ge(scalars_ready, 3)
            dve.tensor_scalar(gqk[:], gqk[:], float(D) ** 0.5, None, ALU.mult).then_inc(scalars_ready, 1)
            dve.wait_ge(scalars_ready, 4)
            uses = Uses(DVE_USES, PAIRS)

            def next_full():
                u = uses.take()
                dve.wait_ge(dve_full, uses.at(u))

            def norm_stats(kind, batch, r, src):
                dve.bn_stats(ln_stats[:, kind, r, :], src).then_inc(bn_ready[kind], 1)
                dve.wait_ge(bn_ready[kind], batch + 1)
                dve.sem_inc(dve_turns, 1)
                dve.bn_aggr(ln_mv[:, kind, r, :], ln_stats[:, kind, r, :]).then_inc(mv_ready[kind], 1)

            def normalise(kind, batch, r, dst, src, done):
                dve.wait_ge(rstd_ready[kind], batch + 1)
                dve.tensor_scalar(dst, src, ln_mv[:, kind, r, 0:1], ln_rstd[:, kind, r, 0:1],
                                  ALU.subtract, ALU.mult).then_inc(done, 1)

            def drain_ctxT(slot, batch):
                for c in range(CC):
                    next_full()
                    dve.tensor_copy(ctxT_hi[:, slot, c, 0:SK], ps_dve[:, 0:SK]).then_inc(ctxT_rounded, 1)
                    dve.wait_ge(ctxT_rounded, CC * batch + c + 1)
                    dve.tensor_tensor(ctxT_lo[:, slot, c, 0:SK], ps_dve[:, 0:SK],
                                      ctxT_hi[:, slot, c, 0:SK].bitcast(fp32), ALU.subtract).then_inc(dve_drained, 1)

            def drain_xT(r):
                next_full()
                dve.tensor_copy(xT[:, :, r, :], ps_dve[:, 0:MC * SQ].rearrange("p (c q) -> p c q", c=MC))\
                   .then_inc(dve_drained, 1)

            def drain_query_sums(group):
                next_full()
                wait_for(dve, rq_ready, group)
                dve.tensor_copy(q_ss[:], ps_dve[0:SQ, 0:2 * GH]).then_inc(dve_drained, 1)
                dve.wait_ge(dve_drained, uses.at(uses.count))
                dve.tensor_scalar(q_se[:], q_ss[:], D * EPS, None, ALU.add).then_inc(qse_ready, 1)

            next_full()
            dve.tensor_copy(gwT[:].rearrange("p c e -> p (c e)"), ps_dve[:, 0:MC * E]).then_inc(dve_drained, 1)
            drain_ctxT(0, 0)
            for r in range(2):
                dve.wait_ge(x_loaded[r], 16)
                norm_stats(0, r, r, x_in[:, r, :])
                normalise(0, r, r, x_in[:, r, :], x_in[:, r, :], xn_ready)
            for r in range(2):
                drain_xT(r)
            dve.wait_ge(wk_loaded, 16)
            dve.tensor_copy(wk_hi[:], wk_whole[:]).then_inc(wk_split, 1)
            dve.wait_ge(wk_split, 1)
            dve.tensor_tensor(wk_lo[:], wk_whole[:], wk_hi[:].bitcast(fp32), ALU.subtract).then_inc(wk_split, 1)
            drain_query_sums(0)

            def steps(s, l):
                p = s.pair
                n = UNITS * p + l
                def maxima(hp):
                    u, g, r = n - 1, (l - 1) % NG, (l - 1) % UNITS // NG
                    dve.wait_ge(s_full, 2 * u + hp + 1)
                    dve.tensor_reduce(s_max[:, hp, :], ps_s[0:SQ, :, 0:SK], X, ALU.max).then_inc(smax_ready, 1)
                    dve.wait_ge(smax_ready, 2 * u + hp + 1)
                    dve.scalar_tensor_tensor(s_bias[:, hp, :], s_max[:, hp, :], -1.0,
                                             rq[:, g, 2 * hp:2 * hp + 2, r], ALU.mult, ALU.mult)\
                       .then_inc(sbias_ready, 1)

                if (l == 7 and s.nxt) or (l in (0, 1, 2) and s.cur):
                    drain_query_sums(NG * p + (l + 1) % UNITS if l < 7 else NG * (p + 1))
                if l == 4 and s.nxt:
                    drain_xT(0)
                for at, rel in ((4, -1), (0, -2)):
                    if l == at and s.batch(rel):
                        next_full()
                        dve.tensor_copy(xn2T[:].rearrange("p c q -> p (c q)"), ps_dve[:, 0:MC * SQ])\
                           .then_inc(dve_drained, 1)
                for at, rel in ((1, -2), (5, -1)):
                    if l == at and s.batch(rel):
                        b, r = 2 * p + rel, rel % 2
                        next_full()
                        dve.tensor_tensor(logits[:, r, :], ps_dve[0:SQ, 0:E], gate_bias[:], ALU.add)\
                           .then_inc(dve_drained, 1)
                        dve.wait_ge(dve_drained, uses.at(uses.count))
                        dve.sem_inc(dve_turns, 1)
                        dve.max(best[:], logits[:, r, :]).then_inc(best_ready, 1)
                        dve.wait_ge(best_ready, 2 * b + 1)
                        dve.sem_inc(dve_turns, 1)
                        dve.max_index(best_index[:], best[:], logits[:, r, :]).then_inc(best_ready, 1)
                        dve.tensor_copy(top_value[:, ds(b, 1), :].rearrange("p o k -> p (o k)"), best[:, 0:TOPK])\
                           .then_inc(top_ready, 1)
                        dve.wait_ge(best_ready, 2 * b + 2)
                        dve.tensor_copy(top_index[:, ds(b, 1), :].rearrange("p o k -> p (o k)"), best_index[:, 0:TOPK])\
                           .then_inc(top_ready, 1)
                if l == 5 and s.nxt:
                    drain_xT(1)
                if (l == 3 and s.cur) or (l == 7 and s.nxt):
                    drain_ctxT((l // NG + 1) % 2, 2 * p + (l + 1) // NG)
                if s.cur:
                    dve.wait_ge(ksq_ready, n + 1)
                    dve.tensor_reduce(k_ss[:], kn[:], X, ALU.add).then_inc(kss_ready, 1)
                if s.unit(l - 1):
                    dve.wait_ge(rq_ready, (NG * p + (l - 1) % NG + 1) if l > 0 else NG * p)
                    maxima(0)
                for at, r in ((2, 0), (3, 1)):
                    if l == at and s.nxt:
                        dve.wait_ge(x_loaded[r], 16 * (p + 2))
                        norm_stats(0, 2 * p + 2 + r, r, x_in[:, r, :])
                if s.cur:
                    dve.wait_ge(rk_ready, n + 1)
                    dve.tensor_tensor(kn[:].rearrange("p t h d -> p (t h) d"),
                                      ps_k[:].rearrange("p t (h d) -> p (t h) d", h=GH),
                                      rk[:].rearrange("p t h -> p (t h)").unsqueeze(2)
                                      .broadcast_to([128, KT * GH, D]), ALU.mult).then_inc(kn_ready, 1)
                for at, r in ((2, 0), (3, 1)):
                    if l == at and s.nxt:
                        normalise(0, 2 * p + 2 + r, r, x_in[:, r, :], x_in[:, r, :], xn_ready)
                if s.unit(l - 2):
                    use = probs_use[s.place, l]
                    dve.wait_ge(act_drained, use + (p - 1) * ACT_USES if s.place == "loop" else use)
                    for rows_, ts in parts:
                        dve.tensor_copy(pT_hi[rows_, ts, :], pT_whole[rows_, ts, :]).then_inc(pT_rounded, 1)
                for at, rel in ((3, -1), (7, 0)):
                    if l == at and s.batch(rel):
                        b, r = 2 * p + rel, rel % 2
                        next_full()
                        dve.wait_ge(xres_loaded[r], 16 * (p + rel // 2 + 1))
                        dve.scalar_tensor_tensor(x1[:, r, :], ps_dve[0:SQ, :], tanh_x[0:SQ, 0:1], x1[:, r, :],
                                                 ALU.mult, ALU.add).then_inc(dve_drained, 1)
                        dve.wait_ge(dve_drained, uses.at(uses.count))
                        norm_stats(1, b, r, x1[:, r, :])
                if s.unit(l - 3):
                    g = (l - 3) % NG
                    next_full()
                    dve.tensor_copy(oT[:, GH * g:GH * g + GH, :].rearrange("p h q -> p (h q)"),
                                    ps_dve[:, 0:GH * SQ]).then_inc(dve_drained, 1)
                if s.unit(l - 1):
                    maxima(1)
                if s.unit(l - 2):
                    dve.wait_ge(pT_rounded, 2 * (n - 2) + 2)
                    for rows_, ts in parts:
                        dve.tensor_tensor(pT_lo[rows_, ts, :], pT_whole[rows_, ts, :],
                                          pT_hi[rows_, ts, :].bitcast(fp32), ALU.subtract).then_inc(pT_split, 1)
                for at, rel in ((3, -1), (7, 0)):
                    if l == at and s.batch(rel):
                        r = rel % 2
                        normalise(1, 2 * p + rel, r, xn2[:, r, :], x1[:, r, :], xn2_ready)

            run(dve, steps, [uses])

            step = [0]

            def then(ins):
                step[0] += 1
                ins.then_inc(picks_done, 1)
                dve.wait_ge(picks_done, step[0])

            dve.wait_ge(top_ready, 2 * B)
            attention_stored(dve)
            then(dve.tensor_copy(chosen[:], top_index[:]))
            then(dve.tensor_tensor(v_gap[:], top_value[:],
                                   top_value[:, :, 0:1].broadcast_to([SQ, B, TOPK]), ALU.subtract))
            dve.wait_ge(moe_consts, 9)
            dve.tensor_copy(iota_e[:], iota_e_i[:]).then_inc(moe_floats, 1)
            dve.tensor_copy(iota_l[:], iota_l_i[:]).then_inc(moe_floats, 1)
            dve.tensor_copy(iota_t[:], iota_t_i[:]).then_inc(moe_floats, 1)
            dve.tensor_copy(token_1[:], token_i[:]).then_inc(moe_floats, 1)
            dve.wait_ge(moe_floats, 4)
            for k in range(TOPK):
                then(dve.tensor_tensor(hot[:, k, :, :], iota_e[0:SQ, :].unsqueeze(1).broadcast_to([SQ, B, E]),
                                       chosen[:, :, k:k + 1].broadcast_to([SQ, B, E]), ALU.is_equal))
            then(dve.tensor_tensor(hot_sum[:], hot[:, 0, :, :], hot[:, 1, :, :], ALU.add))
            then(dve.tensor_tensor(hot_sum[:], hot_sum[:], hot[:, 2, :, :], ALU.add))
            then(dve.tensor_tensor(hot_sum[:], hot_sum[:], hot[:, 3, :, :], ALU.add))
            assert step[0] == HOT_SUM_STEP
            dve.wait_ge(gaps_exp, 1)
            then(dve.tensor_reduce(v_sum[:], v_exp[:], X, ALU.add))
            then(dve.reciprocal(v_inv[:], v_sum[:]))
            then(dve.scalar_tensor_tensor(weight[:], v_exp[:], tanh_f[0:SQ, 0:1],
                                          v_inv[:].broadcast_to([SQ, B, TOPK]), ALU.mult, ALU.mult))
            then(dve.tensor_copy(weight_hi[:], weight[:]))
            then(dve.tensor_tensor(weight_lo[:], weight[:], weight_hi[:].bitcast(fp32), ALU.subtract))
            dve.wait_ge(ranks_full, 2)
            then(dve.tensor_copy(count[:], ps_count.rearrange("p (b e) -> p e b", b=B)))
            then(dve.tensor_tensor_scan(run_sum[:].rearrange("p e b -> p (e b)"),
                                        ones_eb[:].rearrange("p e b -> p (e b)"),
                                        count[:].rearrange("p e b -> p (e b)"), 0.0, ALU.mult, ALU.add))
            then(dve.tensor_tensor(count[:], run_sum[:], count[:], ALU.subtract))
            then(dve.tensor_tensor(n_e[:], run_sum[:, :, B - 1], count[:, :, 0], ALU.subtract))
            then(dve.tensor_scalar(n_e_i[:], n_e[:], 127.0, None, ALU.add))
            then(dve.tensor_scalar(n_t_i[:], n_e_i[:], 7, None, ALU.arith_shift_right))
            then(dve.tensor_copy(n_t[:], n_t_i[:]))
            then(dve.tensor_tensor_scan(t_end[:], ones_eb[:, :, 0], n_t[:], 0.0, ALU.mult, ALU.add))
            then(dve.tensor_tensor(shift[:], t_end[:], n_t[:], ALU.subtract))
            then(dve.scalar_tensor_tensor(shift[:], shift[:], 128.0, count[:, :, 0], ALU.mult, ALU.subtract))
            then(dve.tensor_tensor(count[:], count[:], shift[:].unsqueeze(2).broadcast_to([SQ, E, B]), ALU.add))
            then(dve.tensor_tensor(place[:], ps_rank.rearrange("p (b e) -> p b e", b=B),
                                   count[:].rearrange("p e b -> p b e"), ALU.add))
            for k in range(TOPK):
                then(dve.tensor_tensor(hot_place[:, k, :, :], hot[:, k, :, :], place[:], ALU.mult))
            then(dve.tensor_reduce(slot_f[:], hot_place, X, ALU.add))
            then(dve.tensor_copy(slot_i[:], slot_f[:]))
            then(dve.tensor_scalar(slot_hi_i[:], slot_i[:], 7, None, ALU.arith_shift_right))
            then(dve.tensor_scalar(slot_lo_i[:], slot_i[:], 127, None, ALU.bitwise_and))
            then(dve.tensor_copy(slot_hi[:], slot_hi_i[:]))
            then(dve.tensor_copy(slot_lo[:], slot_lo_i[:]))
            for m in range(TOPK * B):
                k, b, j = m // B, m % B, m % NH
                wait_for(dve, map_step, m - NH + 1)
                dve.tensor_scalar(hot_lo[:, j, :], iota_l[0:SQ, :], slot_lo[:, k, b:b + 1], None, ALU.is_equal)\
                   .then_inc(hots_ready, 1)
                dve.tensor_scalar(hot_val[:, j, 0, :], iota_t[0:SQ, :], slot_hi[:, k, b:b + 1],
                                  token_1[0:SQ, b:b + 1], ALU.is_equal, ALU.mult).then_inc(hots_ready, 1)
                dve.tensor_scalar(hot_hi[:, j, :], iota_t[0:SQ, :], slot_hi[:, k, b:b + 1], None, ALU.is_equal)\
                   .then_inc(hots_ready, 1)
            then(dve.tensor_tensor(tile_cmp, t_end[0:1, :].unsqueeze(1).broadcast_to([1, NT, E]),
                                   iota_t[0:1, :].unsqueeze(2).broadcast_to([1, NT, E]), ALU.is_le))
            then(dve.tensor_reduce(tile_e[:], tile_cmp, X, ALU.add))
            then(dve.tensor_scalar(tile_tab[:, 0, :], tile_e[:], float(E - 1), None, ALU.min))
            then(dve.tensor_scalar(tile_b[:], tile_tab[:, 0, :], NB - 1, None, ALU.bitwise_and))
            then(dve.tensor_copy(tile_b_f[:], tile_b[:]))
            then(dve.tensor_scalar(tile_tab[:, 1, :], tile_b_f[:], float(EW), None, ALU.mult))
            then(dve.tensor_scalar(t_end_i[:], t_end[:], 1.0, None, ALU.add))
            dve.wait_ge(map_step, TOPK * B)
            then(dve.tensor_copy(slot_tok[:], ps_map[:, 0:NT]))
            then(dve.tensor_copy(slot_w[:], ps_map[:, NT:2 * NT]))
            then(dve.tensor_tensor(slot_w[:], slot_w[:], ps_map[:, 2 * NT:3 * NT], ALU.add))
            then(dve.tensor_scalar(gather_i[:], slot_tok[:], -1.0, 0.0, ALU.add, ALU.max))
            then(dve.tensor_scalar(pad_far[:], slot_tok[:], 0.0, float(2 ** 20), ALU.is_equal, ALU.mult))
            then(dve.scalar_tensor_tensor(slot_tok[:], slot_tok[:], -1.0, pad_far[:], ALU.add, ALU.add))
            dve.tensor_copy(scatter_i[:], slot_tok[:]).then_inc(table_ready, 1)

            def stage(j, i, has):
                r = i % 2
                if not has[0]:
                    return
                dve.wait_ge(gu_full, j + 1)
                dve.tensor_scalar(g_min[:, r, :], ps_gu[:, r, 0:F], 7.0, None, ALU.min).then_inc(g_ready, 1)
                dve.tensor_scalar(u_min[:, r, :], ps_gu[:, r, F:2 * F], 1.0, 8.0, ALU.add, ALU.min)\
                   .then_inc(gu_drained, 1)
                dve.wait_ge(sig_ready, j + 1)
                dve.tensor_tensor(glu[:, r, :], g_min[:, r, :], sig[:, r, :], ALU.mult).then_inc(glu_ready, 1)
                dve.wait_ge(glu_ready, j + 1)
                dve.wait_ge(gu_drained, j + 1)
                dve.scalar_tensor_tensor(hid[:, r, :], u_min[:, r, :], -6.0, glu[:, r, :], ALU.max, ALU.mult)\
                   .then_inc(hid_ready, 1)

            expert_tiles(dve, stage)

        @block.tensor
        def _(pe):
            mm = nc.tensor.matmul
            acts, dves = Uses(ACT_USES, PAIRS), Uses(DVE_USES, PAIRS)

            def act_use():
                u = acts.take()
                wait_for(pe, act_drained, acts.at(u - 2))
                return act_bank[u % 2]

            def dve_use():
                u = dves.take()
                wait_for(pe, dve_drained, dves.at(u - 1))
                return ps_dve

            def transpose(dst, src, size):
                return nc.tensor.transpose(dst, src, ident[0:size, 0:size])

            def transpose_ctx(slot, batch_of_slot, c):
                pe.wait_ge(ctx_loaded[slot], 32 * (batch_of_slot + 1))
                bank = dve_use()
                for t in range(KT):
                    rows_ = KROWS[t]
                    last = transpose(bank[:, 128 * t:128 * t + rows_],
                                     ctx_whole[0:rows_, slot, t, 128 * c:128 * c + 128], rows_)
                last.then_inc(dve_full, 1)

            def transpose_x(r, batch):
                pe.wait_ge(xn_ready, batch + 1)
                bank = dve_use()
                for c in range(MC):
                    last = transpose(bank[:, SQ * c:SQ * c + SQ], x_in[:, r, 128 * c:128 * c + 128], SQ)
                last.then_inc(dve_full, 1)

            def queries(g):
                for t in range(2):
                    bank = act_use()
                    for j in range(2):
                        h = GH * g + 2 * t + j
                        for c in range(MC):
                            last = mm(bank[:, 2 * SQ * j:2 * SQ * (j + 1)], wq_sb[:, c, D * h:D * h + D],
                                      xT[:, c, :, :].rearrange("p r q -> p (r q)"), start=(c == 0), stop=(c == MC - 1))
                    last.then_inc(act_full, 1)

            def query_sums():
                pe.wait_ge(act_drained, acts.at(query_uses[-1]))
                bank = dve_use()
                for h in range(GH):
                    for r in range(2):
                        last = mm(bank[0:SQ, 2 * h + r:2 * h + r + 1], q_sq[:, h, SQ * r:SQ * r + SQ], ones_col[:],
                                  start=True, stop=True)
                last.then_inc(dve_full, 1)

            query_uses = []
            pe.wait_ge(consts_ready, 7)
            pe.wait_ge(gatew_loaded, 16)
            bank = dve_use()
            for c in range(MC):
                last = transpose(bank[:, E * c:E * c + E], gwn_sb[:, 128 * c:128 * c + 128], E)
            last.then_inc(dve_full, 1)
            for c in range(CC):
                transpose_ctx(0, 0, c)
            for r in range(2):
                transpose_x(r, r)
            pe.wait_ge(dve_drained, dves.count)
            pe.wait_ge(wq0_loaded, 16)
            queries(0)
            query_uses.append(acts.count)
            query_sums()
            pe.wait_ge(wq_loaded, 16)
            queries(1)
            query_uses.append(acts.count)
            pe.wait_ge(wk_split, 2)
            def steps(s, l):
                p = s.pair
                n = UNITS * p + l
                new, mid, late, old = s.cur, s.unit(l - 1), s.unit(l - 2), s.unit(l - 3)
                mid_g, mid_slot = (l - 1) % NG, (l - 1) % UNITS // NG
                old_g, old_slot = (l - 3) % NG, (l - 3) % UNITS // NG
                kT_uses, mix_uses = [], []

                if s.place == "first" and l == 3:
                    pe.wait_ge(wv_loaded, 16)
                    pe.wait_ge(wo_loaded, 16)

                def raw_keys(t, c):
                    slot, g = l // NG, l % NG
                    for rows_part, weights_part in ((ctxT_hi, wk_lo), (ctxT_hi, wk_hi), (ctxT_lo, wk_hi)):
                        last = mm(ps_k[:, t, :], rows_part[:, slot, c, 128 * t:128 * t + 128],
                                  weights_part[:, c, GH * D * g:GH * D * (g + 1)],
                                  start=(c == 0 and weights_part is wk_lo),
                                  stop=(c == CC - 1 and rows_part is ctxT_lo))
                    if t == KT - 1 and c == CC - 1:
                        last.then_inc(k_full, 1)

                def transpose_xn2(rel):
                    r = rel % 2
                    pe.wait_ge(xn2_ready, 2 * p + rel + 1)
                    bank = dve_use()
                    for c in range(MC):
                        last = transpose(bank[:, SQ * c:SQ * c + SQ], xn2[:, r, 128 * c:128 * c + 128], SQ)
                    last.then_inc(dve_full, 1)

                def gate_logits():
                    bank = dve_use()
                    for c in range(MC):
                        last = mm(bank[0:SQ, 0:E], xn2T[:, c, :], gwT[:, c, :], start=(c == 0), stop=(c == MC - 1))
                    last.then_inc(dve_full, 1)

                def short_uses():
                    if (l == 7 and s.nxt) or (l in (0, 1, 2) and s.cur):
                        yield query_sums
                    if l == 4 and s.nxt:
                        yield lambda: transpose_x(0, 2 * p + 2)
                    for at, rel in ((4, -1), (0, -2)):
                        if l == at and s.batch(rel):
                            yield lambda: transpose_xn2(rel)
                    for at, rel in ((1, -2), (5, -1)):
                        if l == at and s.batch(rel):
                            yield gate_logits
                    if l == 5 and s.nxt:
                        yield lambda: transpose_x(1, 2 * p + 3)
                    if (l == 3 and s.cur) or (l == 7 and s.nxt):
                        slot = (l // NG + 1) % 2
                        for c in range(CC):
                            yield lambda: transpose_ctx(slot, p if slot else p + 1, c)
                        ctx_use[0] = dves.count

                def transpose_probs(t):
                    bank = act_use()
                    for h in range(GH):
                        last = transpose(bank[0:KROWS[t], SQ * h:SQ * h + SQ],
                                         probs[:, h, 128 * t:128 * t + KROWS[t]], SQ)
                        if t == 0 and h == 0 and old and old_g == NG - 1:
                            last.then_inc(ctx_free, 1)
                    last.then_inc(act_full, 1)

                def transpose_keys(h):
                    bank = act_use()
                    for t in range(KT):
                        last = transpose(bank[:, 128 * t:128 * t + KROWS[t]], kn[0:KROWS[t], t, h, :],
                                         KROWS[t])
                    last.then_inc(act_full, 1)
                    kT_uses.append(acts.count)

                def scores(hp):
                    u = n - 1
                    pe.wait_ge(act_drained, acts.at(kT_uses[2 * hp + 1]))
                    wait_for(pe, exp_done, GH * u + 2 * hp)
                    for j in range(2):
                        h = 2 * hp + j
                        last = mm(ps_s[0:SQ, j, 0:SK], qT[:, GH * mid_g + h, mid_slot, :], kT[:, h, :],
                                  start=True, stop=True)
                    last.then_inc(s_full, 1)

                def mix_context(c):
                    bank = act_use()
                    for t in range(KT):
                        for rows_part, probs_part in ((ctx_hi, pT_lo), (ctx_hi, pT_hi), (ctx_lo, pT_hi)):
                            last = mm(bank[:, 0:GH * SQ],
                                      rows_part[0:KROWS[t], old_slot, t, 128 * c:128 * c + 128],
                                      probs_part[0:KROWS[t], t, :], start=(t == 0 and probs_part is pT_lo),
                                      stop=(t == KT - 1 and rows_part is ctx_lo))
                    last.then_inc(act_full, 1)
                    mix_uses.append(acts.count)

                if new:
                    if l in (0, 4):
                        pe.wait_ge(dve_drained, dves.at(ctx_use[0]))
                    wait_for(pe, kn_ready, n)
                short = short_uses()
                for i in range(KT * CC):
                    if new:
                        raw_keys(i // CC, i % CC)
                    if mid and i < GH:
                        if i == 0:
                            pe.wait_ge(kn_ready, n)
                        transpose_keys(i)
                    if i % 2 == 1:
                        next(short, lambda: None)()
                for use in short:
                    use()
                if old:
                    pe.wait_ge(pT_split, 2 * (n - 3) + 2)
                    pe.wait_ge(ctx_split, 4 * (2 * p + (l - 3) // NG) + 4)
                    for c in range(CC):
                        mix_context(c)
                if late:
                    pe.wait_ge(probs_ready, 2 * (n - 2) + 2)
                    transpose_probs(0)
                if mid:
                    scores(0)
                if late:
                    for t in range(1, KT):
                        transpose_probs(t)
                for at, rel in ((3, -1), (7, 0)):
                    if l == at and s.batch(rel):
                        bank = dve_use()
                        for h in range(H):
                            last = mm(bank[0:SQ, :], oT[:, h, :], wo_sb[:, h, :], start=(h == 0), stop=(h == H - 1))
                        last.then_inc(dve_full, 1)
                if (l in (6, 7) and s.nxt) or (l in (0, 1) and s.cur):
                    queries({6: 0, 7: 1, 0: 2, 1: 3}[l])
                    query_uses.append(acts.count)
                output_step = l in (3, 7) and s.batch(l - 7)
                if mid and output_step:
                    scores(1)
                if old:
                    pe.wait_ge(act_drained, acts.at(mix_uses[-1]))
                    bank = dve_use()
                    for h in range(GH):
                        for c in range(CC):
                            last = mm(bank[:, SQ * h:SQ * h + SQ],
                                      wv_sb[:, c, D * (GH * old_g + h):D * (GH * old_g + h + 1)],
                                      mixT[:, c, SQ * h:SQ * h + SQ], start=(c == 0), stop=(c == CC - 1))
                    last.then_inc(dve_full, 1)
                if mid and not output_step:
                    scores(1)

            ctx_use = [dves.count]
            run(pe, steps, [acts, dves])

            pe.wait_ge(picks_done, HOT_SUM_STEP)
            for lhs, dst in ((before, ps_rank), (ones_sq, ps_count)):
                for c in range(0, B * E, 512):
                    w = min(512, B * E - c)
                    last = mm(dst[:, c:c + w], lhs[:], hot_sum[:].rearrange("p b e -> p (b e)")[:, c:c + w],
                              start=True, stop=True)
                last.then_inc(ranks_full, 1)
            for m in range(TOPK * B):
                pe.wait_ge(vals_ready, 2 * m + 2)
                mm(ps_map[:, 0:3 * NT], hot_lo[:, m % NH, :], hot_val[:, m % NH, :, :].rearrange("p a t -> p (a t)"),
                   start=(m == 0), stop=(m == TOPK * B - 1)).then_inc(map_step, 1)

            def transpose_tile(j, i):
                pe.wait_ge(x_gathered[i], 16 // XB * (j - i) + 16)
                wait_for(pe, xT_drained, j)
                for c in range(MC):
                    last = transpose(ps_xT[:, 128 * c:128 * c + 128], x_tile[:, i, 128 * c:128 * c + 128], 128)
                last.then_inc(xT_full, 1)

            wr = w_ring[:].rearrange("p b w -> p (b w)")
            br = b_rows[:].rearrange("s e n -> s (e n)")

            def where(j):
                return (pe.value_load(tile_tab[0:1, 0, ds(j, 1)], min_val=0, max_val=E - 1),
                        pe.value_load(tile_tab[0:1, 1, ds(j, 1)], min_val=0, max_val=(NB - 1) * EW))

            found = []

            def stage(j, i, has):
                r = i % 2
                if has[0]:
                    e, w = found.pop() if i else where(j)
                    pe.wait_ge(w_loaded, 48 * e + 48)
                    pe.wait_ge(xT_drained, j + 1)
                    wait_for(pe, gu_drained, j - 1)
                    mm(ps_gu[:, r, :], ones3[:], br[:, ds(e * (2 * F + DM), 2 * F)], start=True, stop=False)
                    for c in range(MC):
                        last = mm(ps_gu[:, r, :], xT_tile[:, r, c, :], wr[:, ds(w + c * 2 * F, 2 * F)],
                                  start=False, stop=(c == MC - 1))
                    last.then_inc(gu_full, 1)
                if not has[1]:
                    found.append(where(j + 1))
                else:
                    eb, wb = where(j - 1)
                    if has[2] and i < XB - 1:
                        found.append(where(j + 1))
                    pe.wait_ge(hid_ready, j)
                    wait_for(pe, hT_drained, j - 1)
                    for c in range(FC):
                        last = transpose(ps_hT[:, 128 * c:128 * c + 128], hid[:, 1 - r, 128 * c:128 * c + 128], 128)
                    last.then_inc(hT_full, 1)
                if has[2]:
                    transpose_tile(j + 1, (i + 1) % XB)
                if has[1]:
                    wait_for(pe, o_drained, j - 2)
                    mm(ps_o[1 - r][:], ones3[:], br[:, ds(eb * (2 * F + DM) + 2 * F, DM)], start=True, stop=False)
                    pe.wait_ge(hT_drained, j)
                    for c in range(FC):
                        last = mm(ps_o[1 - r][:], hidT[:, 1 - r, c, :], wr[:, ds(wb + MC * 2 * F + c * DM, DM)],
                                  start=False, stop=(c == FC - 1))
                    last.then_inc(o_full, 1)

            pe.wait_ge(table_ready, 1)
            pe.wait_ge(rows_loaded, 16)
            transpose_tile(0, 0)
            expert_tiles(pe, stage)


NAMES = ["x", "ctx_1024", "g_xattn", "g_ffn", "L0_xattn_Wq", "L0_xattn_Wk", "L0_xattn_Wv", "L0_xattn_Wo",
         "L0_xattn_gq", "L0_xattn_gk", "L0_ffn_gate_w", "L0_ffn_gate_b", "L0_ffn_w_gate", "L0_ffn_b_gate",
         "L0_ffn_w_up", "L0_ffn_b_up", "L0_ffn_w_down", "L0_ffn_b_down"]


def kernel(**inputs):
    import numpy as np
    import concourse.bacc as bacc
    from concourse.bass_utils import run_bass_kernel_spmd

    nc = bacc.Bacc("TRN2", target_bir_lowering=False, num_devices=1)
    arrays, args = {}, []
    for name in NAMES:
        a = np.ascontiguousarray(inputs[name])
        arrays[f"in_{name}"] = a
        args.append(nc.dram_tensor(f"in_{name}", a.shape, mybir.dt.from_np(a.dtype), kind="ExternalInput").ap())
    shape = inputs["x"].shape
    args.append(nc.dram_tensor("out", shape, fp32, kind="ExternalOutput").ap())
    flamingo_block(nc, *args)
    r = run_bass_kernel_spmd(nc, [arrays], core_ids=[0])
    return r.results[0]["out"]
```
